# Optimizing a Trainium2 kernel written in Bass

```python
import numpy as np
import jax
import jax.numpy as jnp

def _softmax(x, axis=-1):
    return jax.nn.softmax(x, axis=axis)

def _gelu(x):
    return jax.nn.gelu(x, approximate=True)

def _silu(x):
    return jax.nn.silu(x)

def _sigmoid(x):
    return jax.nn.sigmoid(x)

def _layernorm(x, axis=-1, eps=1e-05):
    m = jnp.mean(x, axis=axis, keepdims=True)
    v = jnp.var(x, axis=axis, keepdims=True)
    return (x - m) / jnp.sqrt(v + eps)

def _scatter_add(tgt, idx, src, axis=0):
    return tgt.at[idx].add(src)

def _segment_sum(src, seg, n):
    return jax.ops.segment_sum(src, seg, n)
kernel_name = 'mk_conv_preact_d1_conv_nchw256_r4_664ca6'

def setup_inputs(seed: int=0):
    np.random.seed(seed)
    _w = jnp.asarray

    def _rec_inputs():
        import jax
        import jax.numpy as jnp
        _gk = jax.random.key(seed)
        x = -0.0003929 + 0.9999 * jax.random.normal(jax.random.fold_in(_gk, 1), (16, 64, 16, 16), jnp.float32)
        return x
    x = _rec_inputs()

    def _L0_conv_setup():
        import jax, jax.numpy as jnp
        import numpy as np
        HEADS = 8
        DIM_HEAD = 16
        DIM = 64
        HIDDEN = HEADS * DIM_HEAD
        EPS = 1e-05

        def group_norm(x, w, b, groups, eps=EPS):
            B, C, H, W = x.shape
            xg = x.reshape(B, groups, C // groups, H, W)
            mu = xg.mean(axis=(2, 3, 4), keepdims=True)
            var = xg.var(axis=(2, 3, 4), keepdims=True)
            xg = (xg - mu) * jax.lax.rsqrt(var + eps)
            x = xg.reshape(B, C, H, W)
            return x * w[None, :, None, None] + b[None, :, None, None]
        key = jax.random.key(seed)
        ks = jax.random.split(key, 4)
        B, H, W = (16, 16, 16)
        x = jax.random.normal(ks[0], (B, DIM, H, W), dtype=jnp.float32)
        qkv_w = jax.random.normal(ks[1], (3 * HIDDEN, DIM), dtype=jnp.float32) * 0.02
        qkv_b = jnp.zeros((3 * HIDDEN,), dtype=jnp.float32)
        out_w = jax.random.normal(ks[2], (DIM, HIDDEN), dtype=jnp.float32) * 0.02
        out_b = jnp.zeros((DIM,), dtype=jnp.float32)
        gn1_w = jnp.ones((DIM,), dtype=jnp.float32)
        gn1_b = jnp.zeros((DIM,), dtype=jnp.float32)
        gn2_w = jnp.ones((DIM,), dtype=jnp.float32)
        gn2_b = jnp.zeros((DIM,), dtype=jnp.float32)
        return {'x': x, 'gn1_w': gn1_w, 'gn1_b': gn1_b, 'qkv_w': qkv_w, 'qkv_b': qkv_b, 'out_w': out_w, 'out_b': out_b, 'gn2_w': gn2_w, 'gn2_b': gn2_b}
    _L0_conv_all = _L0_conv_setup()
    _L0_conv_in = {k: v for k, v in _L0_conv_all.items() if k in ('gn1_w', 'gn1_b', 'qkv_w', 'qkv_b', 'out_w', 'out_b', 'gn2_w', 'gn2_b')}
    del _L0_conv_all
    return {'x': x, 'L0_conv_gn1_w': _L0_conv_in['gn1_w'], 'L0_conv_gn1_b': _L0_conv_in['gn1_b'], 'L0_conv_qkv_w': _L0_conv_in['qkv_w'], 'L0_conv_qkv_b': _L0_conv_in['qkv_b'], 'L0_conv_out_w': _L0_conv_in['out_w'], 'L0_conv_out_b': _L0_conv_in['out_b'], 'L0_conv_gn2_w': _L0_conv_in['gn2_w'], 'L0_conv_gn2_b': _L0_conv_in['gn2_b']}

def reference(x, L0_conv_gn1_w, L0_conv_gn1_b, L0_conv_qkv_w, L0_conv_qkv_b, L0_conv_out_w, L0_conv_out_b, L0_conv_gn2_w, L0_conv_gn2_b):
    import jax
    import jax.numpy as jnp

    def _L0_conv_ref(x, gn1_w, gn1_b, qkv_w, qkv_b, out_w, out_b, gn2_w, gn2_b):
        import jax, jax.numpy as jnp
        import numpy as np
        HEADS = 8
        DIM_HEAD = 16
        DIM = 64
        HIDDEN = HEADS * DIM_HEAD
        EPS = 1e-05

        def group_norm(x, w, b, groups, eps=EPS):
            B, C, H, W = x.shape
            xg = x.reshape(B, groups, C // groups, H, W)
            mu = xg.mean(axis=(2, 3, 4), keepdims=True)
            var = xg.var(axis=(2, 3, 4), keepdims=True)
            xg = (xg - mu) * jax.lax.rsqrt(var + eps)
            x = xg.reshape(B, C, H, W)
            return x * w[None, :, None, None] + b[None, :, None, None]
        B, C, H, W = x.shape
        n = H * W
        scale = DIM_HEAD ** (-0.5)
        res = x
        xn = group_norm(x, gn1_w, gn1_b, 32)
        qkv = jnp.einsum('oc,bchw->bohw', qkv_w, xn) + qkv_b[None, :, None, None]
        q, k, v = jnp.split(qkv, 3, axis=1)
        q = q.reshape(B, HEADS, DIM_HEAD, n) * scale
        k = k.reshape(B, HEADS, DIM_HEAD, n)
        v = v.reshape(B, HEADS, DIM_HEAD, n)
        q_norm = jax.nn.softmax(q, axis=-1)
        k_norm = jax.nn.softmax(k, axis=-2)
        context = jnp.einsum('bhdn,bhen->bhde', k_norm, v)
        out = jnp.einsum('bhde,bhdn->bhen', context, q_norm)
        out = out.reshape(B, HIDDEN, H, W)
        out = jnp.einsum('oc,bchw->bohw', out_w, out) + out_b[None, :, None, None]
        out = group_norm(out, gn2_w, gn2_b, 1)
        return out + res

    def _gn(v, G=32, eps=1e-05):
        B_, C_, H_, W_ = v.shape
        g = v.reshape(B_, G, C_ // G, H_, W_)
        m = jnp.mean(g, axis=(2, 3, 4), keepdims=True)
        s = jnp.var(g, axis=(2, 3, 4), keepdims=True)
        return ((g - m) / jnp.sqrt(s + eps)).reshape(v.shape)

    def _ln_c(v, eps=1e-06):
        m = jnp.mean(v, axis=1, keepdims=True)
        s = jnp.var(v, axis=1, keepdims=True)
        return (v - m) / jnp.sqrt(s + eps)

    def _ln_t(v, eps=1e-05):
        m = jnp.mean(v, axis=-1, keepdims=True)
        s = jnp.var(v, axis=-1, keepdims=True)
        return (v - m) / jnp.sqrt(s + eps)

    def _to_tokens(v):
        B_, C_, H_, W_ = v.shape
        return v.reshape(B_, C_, H_ * W_).transpose(0, 2, 1)

    def _from_tokens(t, like):
        B_, C_, H_, W_ = like.shape
        return t.transpose(0, 2, 1).reshape(B_, C_, H_, W_)
    x = x + _L0_conv_ref(_gn(x), L0_conv_gn1_w, L0_conv_gn1_b, L0_conv_qkv_w, L0_conv_qkv_b, L0_conv_out_w, L0_conv_out_b, L0_conv_gn2_w, L0_conv_gn2_b)
    return x

_drawn_inputs = setup_inputs


def setup_inputs(seed=0):
    import zlib

    import numpy as np

    out = dict(_drawn_inputs(seed))
    spreads = {'L0_conv_gn1_w': (1.0, 0.6),
     'L0_conv_gn1_b': (0.0, 0.507),
     'L0_conv_qkv_b': (0.0, 0.1),
     'L0_conv_out_b': (0.0, 0.1),
     'L0_conv_gn2_w': (1.0, 0.2),
     'L0_conv_gn2_b': (0.0, 0.1)}
    factors = {'L0_conv_qkv_w': 3.233}
    for name, (base, spread) in spreads.items():
        noise = np.random.default_rng([zlib.crc32(name.encode()), seed]).standard_normal(out[name].shape)
        drawn = base * np.exp(spread * noise) if base else spread * noise
        out[name] = jnp.asarray(drawn.astype(out[name].dtype))
    for name, factor in factors.items():
        out[name] = (out[name] * factor).astype(out[name].dtype)
    return out
```

```python
import numpy as np
import concourse.bass as bass
import concourse.mybir as mybir
from contextlib import ExitStack

F32 = mybir.dt.float32
F32R = mybir.dt.float32r
BF16 = mybir.dt.bfloat16
ALU = mybir.AluOpType
ACT = mybir.ActivationFunctionType
AX = mybir.AxisListType

IMAGES, CHANNELS, SIDE = 16, 64, 16
PIX = SIDE * SIDE
HEADS, DIM = 8, 16
HIDDEN = HEADS * DIM
PAIRS = IMAGES // 2
P = 2 * CHANNELS
CHUNKS = PIX // 128
BLOCKS = 2 * CHUNKS
GROUPS = 32
GROUP_CH = CHANNELS // GROUPS
EPS = 1e-5
QSCALE = DIM ** -0.5
FIRST = 2
DMA = 16

GN1_W, GN1_B, OUT_B, GN2_W, GN2_B, PARAMS = range(6)
AVG_GROUP, CENTER, AVG_IMAGE, HEAD_MASK, MATRICES = range(5)


def attention_kernel(nc, x, params, w_qkv_t, b_qkv, w_out_t, matrices, out):
    ctx = ExitStack()
    with ctx:
        def sb(name, shape, dt=F32):
            return ctx.enter_context(nc.sbuf_tensor(name, shape, dt))

        def sem(name):
            return ctx.enter_context(nc.semaphore(name))

        x_sb = sb("x_sb", [P, PAIRS, PIX])
        par = sb("par", [P, PARAMS])
        mats = sb("mats", [P, MATRICES, P])
        w_f = sb("w_f", [P, 3 * HIDDEN])
        w_hi = sb("w_hi", [P, 3 * HIDDEN], F32R)
        w_lo = sb("w_lo", [P, 3 * HIDDEN], F32R)
        wo_sb = sb("wo_sb", [HIDDEN, CHANNELS])
        brow = sb("brow", [1, 3 * HIDDEN])
        brest = sb("brest", [1, 2, 3 * HIDDEN])
        bpart = sb("bpart", [1, 2, 3 * HIDDEN], BF16)
        bsplit = sb("bsplit", [96, 3 * HIDDEN], BF16)
        bsplit_kv = sb("bsplit_kv", [96, CHUNKS, 2 * HIDDEN], BF16)
        ones = sb("ones", [96, 512], BF16)
        xstat = sb("xstat", [P, PAIRS, 6])
        xmv = sb("xmv", [P, PAIRS, 2])
        dev = sb("dev", [P, PAIRS])
        dev2 = sb("dev2", [P, PAIRS])
        gvar = sb("gvar", [P, PAIRS])
        pow_in = sb("pow_in", [P, PAIRS, 2])
        rstd = sb("rstd", [P, PAIRS, 2])
        minus_half = sb("minus_half", [P, 2 * PAIRS])
        coef_a = sb("coef_a", [P, PAIRS])
        mean_a = sb("mean_a", [P, PAIRS])
        coef_b = sb("coef_b", [P, PAIRS])
        coef_p = sb("coef_p", [P, PAIRS])
        mean_r = sb("mean_r", [P, PAIRS])
        rest0 = sb("rest0", [P, PAIRS])
        xn = sb("xn", [P, 2, PIX])
        split = sb("split", [P, 2, 2, PIX], F32R)
        xt = sb("xt", [P, 2, 2, PIX], F32R)
        kmx = sb("kmx", [128, BLOCKS * HEADS])
        ek = sb("ek", [128, 2, BLOCKS * HIDDEN])
        tree = sb("tree", [128, BLOCKS * HEADS, 8])
        tree2 = sb("tree2", [128, BLOCKS * HEADS, 4])
        tree3 = sb("tree3", [128, BLOCKS * HEADS, 2])
        ks = sb("ks", [128, 2, BLOCKS * HEADS])
        rks = sb("rks", [128, BLOCKS * HEADS])
        vs = sb("vs", [128, 2, BLOCKS * HIDDEN])
        nqmax = sb("nqmax", [HIDDEN, 2, 2])
        eq = sb("eq", [HIDDEN, 2, 2, PIX])
        qs = sb("qs", [HIDDEN, 2, 2])
        rq = sb("rq", [HIDDEN, 2, 2])
        ctxm = sb("ctxm", [HIDDEN, 2, HIDDEN])
        fold = sb("fold", [HIDDEN, 2, 2, CHANNELS])
        ostat = sb("ostat", [P, 6])
        omv = sb("omv", [P, 2, 2])
        cdev = sb("cdev", [P, 2])
        msq = sb("msq", [P, 2])
        ve = sb("ve", [P, 2])
        orstd = sb("orstd", [P, 2])
        obc = sb("obc", [P, 1])
        tm = sb("tm", [P, 2])
        coef_q = sb("coef_q", [P, 2])
        coef_r = sb("coef_r", [P, 2])
        tt = sb("tt", [P, 2, PIX])
        res = sb("res", [P, 2, PIX])

        def bank(name, shape):
            return ctx.enter_context(nc.psum_tensor(name, shape, F32))

        kv_ps = [bank(f"kv_ps{u}", [128, BLOCKS, 2, HEADS, DIM]) for u in range(2)]
        q_ps = bank("q_ps", [128, 2, PIX])
        c_ps = bank("c_ps", [128, 512])
        o_ps = [bank(f"o_ps{u}", [128, 512]) for u in range(2)]
        MEAN, VAR = PIX, PIX + 1
        ctx_ps = c_ps[:, 0:2 * HIDDEN]
        fold_ps = c_ps[:, 2 * HIDDEN:2 * HIDDEN + 2 * CHANNELS]

        x_in = [sem(f"x_in{p}") for p in range(PAIRS)]
        par_in, mats_in, w_in, b_in, wo_in = (sem(n) for n in ("par_in", "mats_in", "w_in", "b_in", "wo_in"))
        mats2_in = sem("mats2_in")
        ones_ready = sem("ones_ready")
        w_step = sem("w_step")
        w_ready = sem("w_ready")
        b_step = sem("b_step")
        b_ready = sem("b_ready")
        obc_done, obc_ready = sem("obc_done"), sem("obc_ready")
        xstat_ready, xmv_ready, gavg_done = sem("xstat_ready"), sem("xmv_ready"), sem("gavg_done")
        gn_step, pow_ready, rstd_ready = sem("gn_step"), sem("pow_ready"), sem("rstd_ready")
        coef_ready = sem("coef_ready")
        xn_ready, hi_ready, lo_ready = sem("xn_ready"), sem("hi_ready"), sem("lo_ready")
        xt_in = [sem(f"xt_in{u}") for u in range(2)]
        kv_done, q_done = sem("kv_done"), sem("q_done")
        kmax_ready, ksub_ready, kexp_ready = sem("kmax_ready"), sem("ksub_ready"), sem("kexp_ready")
        tree_step = sem("tree_step")
        ksum_ready, rks_ready, vs_ready = sem("ksum_ready"), sem("rks_ready"), sem("vs_ready")
        qmax_ready, qexp_ready, rq_ready = sem("qmax_ready"), sem("qexp_ready"), sem("rq_ready")
        ctx_done, ctxm_ready, fold_done, fold_ready = (
            sem("ctx_done"), sem("ctxm_ready"), sem("fold_done"), sem("fold_ready"))
        out_done, ostat_ready, omv_ready = sem("out_done"), sem("ostat_ready"), sem("omv_ready")
        cen_done, cdev_ready, msq_ready = sem("cen_done"), sem("cdev_ready"), sem("msq_ready")
        var_done, ve_ready, gn2_step, gn2_ready = (
            sem("var_done"), sem("ve_ready"), sem("gn2_step"), sem("gn2_ready"))
        tm_ready = sem("tm_ready")
        tt_ready, res_ready = sem("tt_ready"), sem("res_ready")
        stored = [sem(f"stored{u}") for u in range(2)]

        def at(j, u, lag):
            return 2 * j + u + lag, (u + lag) % 2, j + (u + lag) // 2

        def there(p):
            return not isinstance(p, int) or 0 <= p < PAIRS

        def wait(eng, semaphore, value):
            if not isinstance(value, int) or value > 0:
                eng.wait_ge(semaphore, value)

        def run_pipeline(eng, step, first, steady, last):
            a, b = steady if LOOPS else (last + 1, last + 1)
            for i in range(first, a):
                step(i // 2, i % 2)
            if b > a:
                with eng.Fori(a // 2, b // 2) as j:
                    for i in (a, a + 1):
                        step(j + (i // 2 - a // 2), i % 2)
            for i in range(b, last + 1):
                step(i // 2, i % 2)

        def of(tensor, p):
            return tensor[:, bass.ds(p, 1)]

        block = ctx.enter_context(nc.Block())

        @block.sync
        def _(sp):
            x_pair = x.rearrange("(p b) c n -> p (b c) n", b=2)
            o_pair = out.rearrange("(p b) c n -> p (b c) n", b=2)
            for p in (0, 1):
                sp.dma_start(x_sb[:, p, :], x_pair[p]).then_inc(x_in[p], DMA)
            for half in range(2):
                sp.dma_start(w_f[half * CHANNELS:(half + 1) * CHANNELS, :], w_qkv_t).then_inc(w_in, DMA)
            for p in (2, 4, 6):
                sp.dma_start(x_sb[:, p, :], x_pair[p]).then_inc(x_in[p], DMA)
            sp.dma_start(wo_sb[:], w_out_t).then_inc(wo_in, DMA)

            def stack(j, u):
                p, r, h = at(j, u, 2)
                if not there(p):
                    return
                wait(sp, lo_ready, p + 1)
                wait(sp, q_done, p - 1)
                for image in range(2):
                    rows = slice(image * CHANNELS, (image + 1) * CHANNELS)
                    for part in range(2):
                        sp.dma_start(
                            xt[part * CHANNELS:(part + 1) * CHANNELS, r, image, :].bitcast(F32),
                            split[rows, r, part, :].bitcast(F32)).then_inc(xt_in[r], DMA)

            def store(j, u):
                p, r, h = at(j, u, -4)
                if not there(p):
                    return
                wait(sp, res_ready, p + 1)
                sp.dma_start(o_pair[p], res[:, r, :]).then_inc(stored[r], DMA)

            def step(j, u):
                stack(j, u)
                store(j, u)

            run_pipeline(sp, step, -2, (4, 6), PAIRS + 3)
            for u in range(2):
                sp.wait_ge(stored[u], DMA * PAIRS // 2)

        @block.gpsimd
        def _(pool):
            nc.gpsimd.memset(minus_half[:], -0.5)
            nc.gpsimd.memset(bsplit[:], 0.0)
            nc.gpsimd.memset(ones[:], 1.0).then_inc(ones_ready, 1)

            def group_rstd(g, a, b):
                pool.wait_ge(pow_ready, g + 1)
                nc.gpsimd.tensor_tensor(
                    rstd[:, a:b, :], pow_in[:, a:b, :],
                    minus_half[:, 2 * a:2 * b].rearrange("p (a t) -> p a t", t=2),
                    ALU.pow).then_inc(rstd_ready, 1)

            def low_part(j, u):
                p, r, h = at(j, u, 2)
                if not there(p):
                    return
                wait(pool, hi_ready, p + 1)
                nc.gpsimd.tensor_tensor(split[:, r, 1, :], xn[:, r, :], split[:, r, 0, :].bitcast(F32),
                                        ALU.subtract).then_inc(lo_ready, 1)

            def key_sums(j, u):
                p, r, h = at(j, u, 0)
                if not there(p):
                    return
                wait(pool, kexp_ready, p + 1)
                wait(pool, tree_step, 3 * p)
                e = ek[:, r, :].rearrange("p (g d) -> p g d", d=DIM)
                nc.gpsimd.tensor_tensor(tree[:], e[:, :, 0:8], e[:, :, 8:16], ALU.add).then_inc(tree_step, 1)
                pool.wait_ge(tree_step, 3 * p + 1)
                nc.gpsimd.tensor_tensor(tree2[:], tree[:, :, 0:4], tree[:, :, 4:8],
                                        ALU.add).then_inc(tree_step, 1)
                pool.wait_ge(tree_step, 3 * p + 2)
                wait(pool, ksum_ready, p)
                nc.gpsimd.tensor_tensor(tree3[:], tree2[:, :, 0:2], tree2[:, :, 2:4],
                                        ALU.add).then_inc(tree_step, 1)
                pool.wait_ge(tree_step, 3 * p + 3)
                wait(pool, rks_ready, p - 1)
                nc.gpsimd.tensor_tensor(ks[:, r, :], tree3[:, :, 0], tree3[:, :, 1],
                                        ALU.add).then_inc(ksum_ready, 1)

            def gn2_coefficients(j, u):
                p, r, h = at(j, u, -4)
                if not there(p):
                    return
                wait(pool, ve_ready, p + 1)
                wait(pool, tm_ready, p + 1)
                wait(pool, tt_ready, p - 1)
                nc.gpsimd.tensor_tensor(orstd[:, r:r + 1], ve[:, r:r + 1], minus_half[:, 0:1],
                                        ALU.pow).then_inc(gn2_step, 1)
                pool.wait_ge(gn2_step, 2 * p + 1)
                nc.gpsimd.tensor_tensor(coef_q[:, r:r + 1], orstd[:, r:r + 1], par[:, GN2_W:GN2_W + 1],
                                        ALU.mult).then_inc(gn2_step, 1)
                pool.wait_ge(gn2_step, 2 * p + 2)
                nc.gpsimd.tensor_scalar(coef_r[:, r:r + 1], tm[:, r:r + 1], coef_q[:, r:r + 1],
                                        of(rest0, p), ALU.mult, ALU.add).then_inc(gn2_ready, 1)

            def step(j, u):
                gn2_coefficients(j, u)
                low_part(j, u)
                key_sums(j, u)

            pool.wait_ge(par_in, DMA)
            pool.wait_ge(ones_ready, 1)
            group_rstd(0, 0, FIRST)
            step(-1, 0)
            step(-1, 1)
            group_rstd(1, FIRST, PAIRS)
            run_pipeline(pool, step, 0, (4, 6), PAIRS + 3)

        @block.scalar
        def _(act):
            x_pair = x.rearrange("(p b) c n -> p (b c) n", b=2)
            act.dma_start(mats[:, AVG_GROUP, :], matrices[:, AVG_GROUP, :]).then_inc(mats_in, DMA)
            act.dma_start(par[:], params).then_inc(par_in, DMA)
            act.dma_start(brow[:], b_qkv).then_inc(b_in, DMA)
            for p in (3, 5, 7):
                act.dma_start(x_sb[:, p, :], x_pair[p]).then_inc(x_in[p], DMA)
            act.dma_start(mats[:, CENTER:MATRICES, :], matrices[:, CENTER:MATRICES, :]).then_inc(mats2_in, DMA)
            act.preload_act_table(ACT.Exp)

            def split_weights():
                act.wait_ge(w_step, 1)
                nc.scalar.activation(w_hi[:], w_f[:], ACT.Copy).then_inc(w_step, 1)

            def affine(j, u):
                p, r, h = at(j, u, 2)
                if not there(p):
                    return
                wait(act, coef_ready, 1 if isinstance(p, int) and p < FIRST else 2)
                wait(act, lo_ready, p - 1)
                nc.scalar.activation(xn[:, r, :], x_sb[:, p, :], ACT.Identity, bias=of(coef_b, p),
                                     scale=of(coef_a, p)).then_inc(xn_ready, 1)

            def high_part(j, u):
                p, r, h = at(j, u, 2)
                if not there(p):
                    return
                wait(act, xn_ready, p + 1)
                wait(act, xt_in[r], 4 * DMA * h)
                nc.scalar.activation(split[:, r, 0, :], xn[:, r, :], ACT.Copy).then_inc(hi_ready, 1)

            def key_exp(j, u):
                p, r, h = at(j, u, 0)
                if not there(p):
                    return
                wait(act, ksub_ready, p + 1)
                nc.scalar.activation(ek[:, r, :], ek[:, r, :], ACT.Exp).then_inc(kexp_ready, 1)

            def query_exp(j, u):
                p, r, h = at(j, u, 0)
                if not there(p):
                    return
                wait(act, qmax_ready, p + 1)
                wait(act, out_done, p - 1)
                wait(act, rq_ready, p - 1)
                for image in range(2):
                    last = nc.scalar.activation(eq[:, r, image, :], q_ps[:, image, :], ACT.Exp,
                                                bias=nqmax[:, r, image:image + 1],
                                                accum_out=qs[:, r, image:image + 1])
                last.then_inc(qexp_ready, 1)

            def fold_copy(j, u):
                p, r, h = at(j, u, -2)
                if not there(p):
                    return
                wait(act, fold_done, p + 1)
                wait(act, rq_ready, p + 1)
                wait(act, out_done, p - 1)
                for image in range(2):
                    last = nc.scalar.activation(fold[:, r, image, :],
                                                fold_ps[:, image * CHANNELS:(image + 1) * CHANNELS],
                                                ACT.Copy, scale=rq[:, r, image:image + 1])
                last.then_inc(fold_ready, 1)

            def normalise(j, u):
                p, r, h = at(j, u, -4)
                if not there(p):
                    return
                wait(act, gn2_ready, p + 1)
                wait(act, res_ready, p - 1)
                nc.scalar.activation(tt[:, r, :], o_ps[r][:, 0:PIX], ACT.Identity,
                                     bias=coef_r[:, r:r + 1], scale=coef_q[:, r:r + 1]).then_inc(tt_ready, 1)

            def step(j, u):
                affine(j, u)
                high_part(j, u)
                normalise(j, u)
                fold_copy(j, u)
                key_exp(j, u)
                query_exp(j, u)

            step(-1, 0)
            split_weights()
            step(-1, 1)
            run_pipeline(act, step, 0, (4, 6), PAIRS + 3)

        @block.tensor
        def _(pe):
            def group_average(g, a, b):
                pe.wait_ge(xmv_ready, g + 1)
                nc.tensor.matmul(o_ps[g][:, 0:2 * (b - a)], mats[:, AVG_GROUP, :],
                                 xmv[:, a:b, :], start=True, stop=True).then_inc(gavg_done, 1)

            def keys_values(j, u):
                p, r, h = at(j, u, 1)
                if not there(p):
                    return
                wait(pe, xt_in[r], 4 * DMA * (h + 1))
                wait(pe, vs_ready, p - 1)
                for image in range(2):
                    nc.tensor.matmul(kv_ps[r][:, image * CHUNKS:(image + 1) * CHUNKS, :, :, :],
                                     ones[:, 0:128], bsplit_kv[:], start=True, stop=False,
                                     skip_group_check=True)
                    for chunk in range(CHUNKS):
                        pixels = xt[:, r, image, chunk * 128:(chunk + 1) * 128]
                        for w in (w_hi, w_lo):
                            ins = nc.tensor.matmul(kv_ps[r][:, image * CHUNKS + chunk, :, :, :], pixels,
                                                   w[:, HIDDEN:3 * HIDDEN], start=False,
                                                   stop=(chunk == CHUNKS - 1 and w is w_lo),
                                                   skip_group_check=True)
                ins.then_inc(kv_done, 1)

            def queries(j, u):
                p, r, h = at(j, u, 0)
                if not there(p):
                    return
                wait(pe, xt_in[r], 4 * DMA * (h + 1))
                wait(pe, qexp_ready, p)
                nc.tensor.matmul(q_ps[:, :, :], bsplit[:, 0:HIDDEN],
                                 ones[:].rearrange("p (i n) -> p i n", i=2), start=True, stop=False,
                                 skip_group_check=True)
                for w in (w_hi, w_lo):
                    ins = nc.tensor.matmul(q_ps[:, :, :], w[:, 0:HIDDEN], xt[:, r, :, :], start=False,
                                           stop=(w is w_lo), skip_group_check=True)
                ins.then_inc(q_done, 1)

            def context(j, u):
                p, r, h = at(j, u, -1)
                if not there(p):
                    return
                wait(pe, vs_ready, p + 1)
                wait(pe, fold_ready, p)
                for blk in range(BLOCKS):
                    image, chunk = divmod(blk, CHUNKS)
                    cols = slice(blk * HIDDEN, (blk + 1) * HIDDEN)
                    ins = nc.tensor.matmul(ctx_ps[:, image * HIDDEN:(image + 1) * HIDDEN],
                                           vs[:, r, cols], ek[:, r, cols],
                                           start=(blk == 0), stop=(chunk == CHUNKS - 1), skip_group_check=True)
                ins.then_inc(ctx_done, 1)

            def folds(j, u):
                p, r, h = at(j, u, -2)
                if not there(p):
                    return
                wait(pe, ctxm_ready, p + 1)
                for image in range(2):
                    ins = nc.tensor.matmul(fold_ps[:, image * CHANNELS:(image + 1) * CHANNELS],
                                           ctxm[:, image, :], wo_sb[:], start=False, stop=True,
                                           skip_group_check=True)
                ins.then_inc(fold_done, 1)

            def outputs(j, u):
                p, r, h = at(j, u, -2)
                if not there(p):
                    return
                wait(pe, fold_ready, p + 1)
                wait(pe, tt_ready, p - 1)
                for image in range(2):
                    ins = nc.tensor.matmul(o_ps[r][image * CHANNELS:(image + 1) * CHANNELS, 0:PIX],
                                           fold[:, r, image, :], eq[:, r, image, :], start=True, stop=True)
                ins.then_inc(out_done, 1)

            def centre(j, u):
                p, r, h = at(j, u, -3)
                if not there(p):
                    return
                wait(pe, omv_ready, p + 1)
                nc.tensor.matmul(o_ps[r][:, MEAN:MEAN + 1], mats[:, CENTER, :], omv[:, r, 0:1],
                                 start=True, stop=True).then_inc(cen_done, 1)

            def variance(j, u):
                p, r, h = at(j, u, -3)
                if not there(p):
                    return
                wait(pe, msq_ready, p + 1)
                nc.tensor.matmul(o_ps[r][:, VAR:VAR + 1], mats[:, AVG_IMAGE, :], msq[:, r:r + 1],
                                 start=True, stop=True).then_inc(var_done, 1)

            def step(j, u):
                queries(j, u)
                centre(j, u)
                folds(j, u)
                outputs(j, u)
                keys_values(j, u)
                variance(j, u)
                context(j, u)

            pe.wait_ge(mats_in, DMA)
            group_average(0, 0, FIRST)
            group_average(1, FIRST, PAIRS)
            pe.wait_ge(mats2_in, DMA)
            pe.wait_ge(par_in, DMA)
            nc.tensor.matmul(c_ps[:, 0:1], mats[:, CENTER, :], par[:, OUT_B:OUT_B + 1],
                             start=True, stop=True).then_inc(obc_done, 1)
            pe.wait_ge(obc_ready, 1)
            pe.wait_ge(ones_ready, 1)
            pe.wait_ge(b_ready, 4)
            pe.wait_ge(w_ready, 1)
            pe.wait_ge(wo_in, DMA)
            run_pipeline(pe, step, -1, (3, 7), PAIRS + 2)

        @block.vector
        def _(dve):
            def pair_stats(p):
                dve.wait_ge(x_in[p], DMA)
                nc.vector.bn_stats(xstat[:, p, :], x_sb[:, p, :]).then_inc(xstat_ready, 1)

            def group_norm(g, a, b):
                for p in range(a, b):
                    pair_stats(p)
                for p in range(a, b):
                    dve.wait_ge(xstat_ready, p + 1)
                    ins = nc.vector.bn_aggr(xmv[:, p, :], xstat[:, p, :])
                ins.then_inc(xmv_ready, 1)
                n = b - a
                avg = o_ps[g][:, 0:2 * n].rearrange("p (a t) -> p a t", t=2)
                s = GN_STEPS * g
                dve.wait_ge(gavg_done, g + 1)
                nc.vector.tensor_tensor(dev[:, a:b], xmv[:, a:b, 0], avg[:, :, 0],
                                        ALU.subtract).then_inc(gn_step, 1)
                dve.wait_ge(gn_step, s + 1)
                nc.vector.tensor_tensor(dev2[:, a:b], dev[:, a:b], dev[:, a:b], ALU.mult).then_inc(gn_step, 1)
                dve.wait_ge(gn_step, s + 2)
                nc.vector.tensor_tensor(gvar[:, a:b], dev2[:, a:b], avg[:, :, 1], ALU.add).then_inc(gn_step, 1)
                dve.wait_ge(gn_step, s + 3)
                nc.vector.tensor_scalar(pow_in[:, a:b, 0], gvar[:, a:b], EPS, None, ALU.add)
                nc.vector.tensor_scalar(pow_in[:, a:b, 1], gvar[:, a:b], 1.0 + EPS, EPS * EPS,
                                        ALU.mult, ALU.add).then_inc(pow_ready, 1)
                dve.wait_ge(rstd_ready, g + 1)
                dve.wait_ge(par_in, DMA)
                nc.vector.tensor_scalar(coef_a[:, a:b], rstd[:, a:b, 1], par[:, GN1_W:GN1_W + 1], None,
                                        ALU.mult).then_inc(gn_step, 1)
                nc.vector.tensor_scalar(coef_p[:, a:b], rstd[:, a:b, 0], 1.0, None, ALU.add)
                nc.vector.tensor_tensor(mean_r[:, a:b], rstd[:, a:b, 0], avg[:, :, 0],
                                        ALU.mult).then_inc(gn_step, 1)
                dve.wait_ge(gn_step, s + 5)
                nc.vector.tensor_tensor(mean_a[:, a:b], coef_a[:, a:b], avg[:, :, 0],
                                        ALU.mult).then_inc(gn_step, 1)
                nc.vector.tensor_scalar(rest0[:, a:b], mean_r[:, a:b], -1.0, par[:, GN2_B:GN2_B + 1],
                                        ALU.mult, ALU.add)
                dve.wait_ge(gn_step, s + 6)
                nc.vector.tensor_scalar(coef_b[:, a:b], mean_a[:, a:b], -1.0, par[:, GN1_B:GN1_B + 1],
                                        ALU.mult, ALU.add).then_inc(coef_ready, 1)

            def prepare_bias():
                dve.wait_ge(b_in, DMA)
                dve.wait_ge(ones_ready, 1)
                nc.vector.tensor_scalar(brow[:, 0:HIDDEN], brow[:, 0:HIDDEN], QSCALE, None,
                                        ALU.mult).then_inc(b_step, 1)
                dve.wait_ge(b_step, 1)
                nc.vector.tensor_copy(bsplit[0:1, :], brow[:]).then_inc(b_ready, 1)
                dve.wait_ge(b_ready, 1)
                nc.vector.tensor_tensor(brest[:, 0, :], brow[:], bsplit[0:1, :], ALU.subtract).then_inc(b_step, 1)
                dve.wait_ge(b_step, 2)
                nc.vector.tensor_copy(bpart[:, 0, :], brest[:, 0, :]).then_inc(b_step, 1)
                nc.vector.tensor_copy(bsplit[32:33, :], brest[:, 0, :]).then_inc(b_ready, 1)
                dve.wait_ge(b_step, 3)
                nc.vector.tensor_tensor(brest[:, 1, :], brest[:, 0, :], bpart[:, 0, :],
                                        ALU.subtract).then_inc(b_step, 1)
                dve.wait_ge(b_step, 4)
                nc.vector.tensor_copy(bsplit[64:65, :], brest[:, 1, :]).then_inc(b_ready, 1)
                dve.wait_ge(b_ready, 3)
                nc.vector.tensor_copy(bsplit_kv[:],
                                      bsplit[:, HIDDEN:3 * HIDDEN].unsqueeze(1).broadcast_to(
                                          [96, CHUNKS, 2 * HIDDEN])).then_inc(b_ready, 1)

            def prepare_weights():
                dve.wait_ge(w_in, 2 * DMA)
                nc.vector.tensor_scalar(w_f[:, 0:HIDDEN], w_f[:, 0:HIDDEN], QSCALE, None,
                                        ALU.mult).then_inc(w_step, 1)
                dve.wait_ge(w_step, 2)
                nc.vector.tensor_tensor(w_lo[:], w_f[:], w_hi[:].bitcast(F32), ALU.subtract).then_inc(w_ready, 1)

            def keys_of(r):
                return kv_ps[r][:, :, 0, :, :]

            def values_of(r):
                return kv_ps[r][:, :, 1, :, :]

            def per_head(t):
                return t.rearrange("p (b g d) -> p b g d", b=BLOCKS, g=HEADS)

            def spread(t):
                return t.rearrange("p (b g) -> p b g", b=BLOCKS).unsqueeze(3).broadcast_to(
                    [128, BLOCKS, HEADS, DIM])

            def key_max(j, u):
                p, r, h = at(j, u, 0)
                if not there(p):
                    return
                wait(dve, kv_done, p + 1)
                wait(dve, ksub_ready, p)
                nc.vector.tensor_reduce(kmx[:], keys_of(r), AX.X, ALU.max).then_inc(kmax_ready, 1)

            def key_shift(j, u):
                p, r, h = at(j, u, 0)
                if not there(p):
                    return
                wait(dve, kmax_ready, p + 1)
                wait(dve, ctx_done, p - 1)
                nc.vector.tensor_tensor(per_head(ek[:, r, :]), keys_of(r), spread(kmx[:]),
                                        ALU.subtract).then_inc(ksub_ready, 1)

            def query_max(j, u):
                p, r, h = at(j, u, 0)
                if not there(p):
                    return
                wait(dve, q_done, p + 1)
                nc.vector.tensor_reduce(nqmax[:, r, :], q_ps[:, :, :], AX.X, ALU.max,
                                        negate=True).then_inc(qmax_ready, 1)

            def key_norm(j, u):
                p, r, h = at(j, u, -1)
                if not there(p):
                    return
                wait(dve, ksum_ready, p + 1)
                wait(dve, vs_ready, p)
                nc.vector.reciprocal(rks[:], ks[:, r, :]).then_inc(rks_ready, 1)

            def scale_values(j, u):
                p, r, h = at(j, u, -1)
                if not there(p):
                    return
                wait(dve, rks_ready, p + 1)
                wait(dve, ctx_done, p - 1)
                nc.vector.tensor_tensor(per_head(vs[:, r, :]), values_of(r), spread(rks[:]),
                                        ALU.mult).then_inc(vs_ready, 1)

            def mask_context(j, u):
                p, r, h = at(j, u, -2)
                if not there(p):
                    return
                wait(dve, qexp_ready, p + 1)
                wait(dve, fold_ready, p - 1)
                nc.vector.reciprocal(rq[:, r, :], qs[:, r, :]).then_inc(rq_ready, 1)
                wait(dve, ctx_done, p + 1)
                wait(dve, fold_done, p)
                nc.vector.tensor_tensor(ctxm[:], ctx_ps.rearrange("p (i d) -> p i d", i=2),
                                        mats[:, HEAD_MASK, :].unsqueeze(1).broadcast_to([P, 2, HIDDEN]),
                                        ALU.mult).then_inc(ctxm_ready, 1)

            def output_stats(j, u):
                p, r, h = at(j, u, -2)
                if not there(p):
                    return
                wait(dve, out_done, p + 1)
                wait(dve, omv_ready, p)
                nc.vector.bn_stats(ostat[:], o_ps[r][:, 0:PIX]).then_inc(ostat_ready, 1)

            def output_moments_waits(j, u):
                p, r, h = at(j, u, -2)
                if not there(p):
                    return
                wait(dve, ostat_ready, p + 1)
                wait(dve, tm_ready, p - 1)

            def output_moments(j, u):
                p, r, h = at(j, u, -2)
                if not there(p):
                    return
                nc.vector.bn_aggr(omv[:, r, :], ostat[:]).then_inc(omv_ready, 1)

            def deviation(j, u):
                p, r, h = at(j, u, -3)
                if not there(p):
                    return
                wait(dve, cen_done, p + 1)
                nc.vector.tensor_tensor(cdev[:, r:r + 1], o_ps[r][:, MEAN:MEAN + 1], obc[:],
                                        ALU.add).then_inc(cdev_ready, 1)

            def squared_deviation(j, u):
                p, r, h = at(j, u, -3)
                if not there(p):
                    return
                wait(dve, cdev_ready, p + 1)
                nc.vector.scalar_tensor_tensor(out=msq[:, r:r + 1], in0=cdev[:, r:r + 1],
                                               scalar=cdev[:, r:r + 1], in1=omv[:, r, 1:2],
                                               op0=ALU.mult, op1=ALU.add).then_inc(msq_ready, 1)
                nc.vector.tensor_tensor(tm[:, r:r + 1], cdev[:, r:r + 1], omv[:, r, 0:1],
                                        ALU.subtract).then_inc(tm_ready, 1)

            def variance_eps(j, u):
                p, r, h = at(j, u, -4)
                if not there(p):
                    return
                wait(dve, var_done, p + 1)
                nc.vector.tensor_scalar(ve[:, r:r + 1], o_ps[r][:, VAR:VAR + 1], EPS, None, ALU.add).then_inc(ve_ready, 1)

            def finish(j, u):
                p, r, h = at(j, u, -4)
                if not there(p):
                    return
                wait(dve, tt_ready, p + 1)
                wait(dve, stored[r], DMA * h)
                nc.vector.scalar_tensor_tensor(out=res[:, r, :], in0=x_sb[:, p, :], scalar=of(coef_p, p),
                                               in1=tt[:, r, :], op0=ALU.mult,
                                               op1=ALU.add).then_inc(res_ready, 1)

            def step(j, u):
                key_max(j, u)
                variance_eps(j, u)
                key_norm(j, u)
                mask_context(j, u)
                key_shift(j, u)
                scale_values(j, u)
                deviation(j, u)
                query_max(j, u)
                squared_deviation(j, u)
                output_stats(j, u)
                output_moments_waits(j, u)
                finish(j, u)
                output_moments(j, u)

            group_norm(0, 0, FIRST)
            prepare_weights()
            prepare_bias()
            group_norm(1, FIRST, PAIRS)
            dve.wait_ge(obc_done, 1)
            nc.vector.tensor_copy(obc[:], c_ps[:, 0:1]).then_inc(obc_ready, 1)
            dve.wait_ge(obc_ready, 1)
            run_pipeline(dve, step, 0, (4, 8), PAIRS + 3)


GN_STEPS = 6
LOOPS = True


def kernel(**inputs):
    import concourse.bacc as bacc
    from concourse.bass_utils import run_bass_kernel_spmd

    arr = {k: np.ascontiguousarray(v) for k, v in inputs.items()}
    names = ("gn1_w", "gn1_b", "out_b", "gn2_w", "gn2_b")
    params = np.stack([np.concatenate([arr["L0_conv_" + n]] * 2) for n in names], axis=1)
    c = np.arange(P)
    group = (c[:, None] // GROUP_CH == c[None, :] // GROUP_CH) / GROUP_CH
    image = (c[:, None] // CHANNELS == c[None, :] // CHANNELS) / CHANNELS
    heads = c[:, None] // DIM == c[None, :] // DIM
    matrices = np.stack([group, np.eye(P) - image, image, heads], axis=1).astype(np.float32)
    data = {
        "x": arr["x"].reshape(IMAGES, CHANNELS, PIX),
        "params": np.ascontiguousarray(params),
        "w_qkv_t": np.ascontiguousarray(arr["L0_conv_qkv_w"].T),
        "b_qkv": arr["L0_conv_qkv_b"].reshape(1, 3 * HIDDEN),
        "w_out_t": np.ascontiguousarray(arr["L0_conv_out_w"].T),
        "matrices": matrices,
    }
    nc = bacc.Bacc("TRN2", target_bir_lowering=False, num_devices=1)
    args = [nc.dram_tensor(n + "_dram", a.shape, mybir.dt.from_np(a.dtype), kind="ExternalInput").ap()
            for n, a in data.items()]
    out = nc.dram_tensor("out_dram", (IMAGES, CHANNELS, PIX), F32, kind="ExternalOutput").ap()
    attention_kernel(nc, *args, out)
    r = run_bass_kernel_spmd(nc, [{n + "_dram": a for n, a in data.items()}], core_ids=[0])
    return r.results[0]["out_dram"].reshape(IMAGES, CHANNELS, SIDE, SIDE)
```

```python
import numpy as np
import concourse.bass as bass
import concourse.mybir as mybir
from contextlib import ExitStack

F32 = mybir.dt.float32
F32R = mybir.dt.float32r
ALU = mybir.AluOpType
ACT = mybir.ActivationFunctionType
AX = mybir.AxisListType

IMAGES, CHANNELS, SIDE = 16, 64, 16
PIX = SIDE * SIDE
HEADS, DIM = 8, 16
HIDDEN = HEADS * DIM
PAIRS = IMAGES // 2
P = 2 * CHANNELS
CHUNKS = PIX // 128
BLOCKS = 2 * CHUNKS
GROUPS = 32
GROUP_CH = CHANNELS // GROUPS
EPS = 1e-5
QSCALE = DIM ** -0.5
NORMED = ((0, 1), (1, 4), (4, 8))
LOADS = ((0, 1), (1, 4), (4, 8))
DIRECT = 2
DMA = 16

GN1_W, GN1_B, OUT_B, GN2_W, GN2_B, PARAMS = range(6)
CENTER, AVG_IMAGE, HEAD_MASK, MATRICES = range(4)


def attention_kernel(nc, x, params, weights, b_qkv, matrices, out):
    ctx = ExitStack()
    with ctx:
        def sb(name, shape, dt=F32):
            return ctx.enter_context(nc.sbuf_tensor(name, shape, dt))

        def sem(name):
            return ctx.enter_context(nc.semaphore(name))

        x_sb = sb("x_sb", [P, PAIRS, PIX])
        par_avg = sb("par_avg", [P, PARAMS + P])
        par, avg_group = par_avg[:, 0:PARAMS], par_avg[:, PARAMS:PARAMS + P]
        mats = sb("mats", [P, MATRICES, P])
        w_all = sb("w_all", [P, 3 * HIDDEN + CHANNELS])
        w_f, wo_sb = w_all[:, 0:3 * HIDDEN], w_all[:, 3 * HIDDEN:]
        w_hi = sb("w_hi", [P, 3 * HIDDEN], F32R)
        w_lo = sb("w_lo", [P, 3 * HIDDEN], F32R)
        brow = sb("brow", [P, 3 * HIDDEN])
        bsplit = sb("bsplit", [P, 3 * HIDDEN], F32R)
        ones = sb("ones", [P, 512], F32R)
        xstat = sb("xstat", [P, PAIRS, 6])
        xmv = sb("xmv", [P, PAIRS, 2])
        dev = sb("dev", [P, PAIRS])
        dev2 = sb("dev2", [P, PAIRS])
        gvar = sb("gvar", [P, PAIRS])
        pow_in = sb("pow_in", [P, PAIRS, 2])
        rstd = sb("rstd", [P, PAIRS, 2])
        minus_half = sb("minus_half", [P, 2 * PAIRS])
        coef_a = sb("coef_a", [P, PAIRS])
        mean_a = sb("mean_a", [P, PAIRS])
        coef_b = sb("coef_b", [P, PAIRS])
        coef_p = sb("coef_p", [P, PAIRS])
        mean_r = sb("mean_r", [P, PAIRS])
        rest0 = sb("rest0", [P, PAIRS])
        xn = sb("xn", [P, 2, PIX])
        split = sb("split", [P, 2, 2, PIX], F32R)
        xt = sb("xt", [P, 2, 2, PIX], F32R)
        kmx = sb("kmx", [128, BLOCKS * HEADS])
        ek = sb("ek", [128, 2, BLOCKS * HIDDEN])
        tree = sb("tree", [128, BLOCKS * HEADS, 8])
        tree2 = sb("tree2", [128, BLOCKS * HEADS, 4])
        tree3 = sb("tree3", [128, BLOCKS * HEADS, 2])
        ks = sb("ks", [128, 2, BLOCKS * HEADS])
        rks = sb("rks", [128, BLOCKS * HEADS])
        vs = sb("vs", [128, 2, BLOCKS * HIDDEN])
        nqmax = sb("nqmax", [HIDDEN, 2, 2])
        eq = sb("eq", [HIDDEN, 2, 2, PIX])
        qs = sb("qs", [HIDDEN, 2, 2])
        rq = sb("rq", [HIDDEN, 2, 2])
        ctxm = sb("ctxm", [HIDDEN, 2, HIDDEN])
        fold = sb("fold", [HIDDEN, 2, 2, CHANNELS])
        ostat = sb("ostat", [P, 6])
        omv = sb("omv", [P, 2, 2])
        cdev = sb("cdev", [P, 2])
        msq = sb("msq", [P, 2])
        ve = sb("ve", [P, 2])
        orstd = sb("orstd", [P, 2])
        obc = sb("obc", [P, 1])
        tm = sb("tm", [P, 2])
        coef_q = sb("coef_q", [P, 2])
        coef_r = sb("coef_r", [P, 2])
        tt = sb("tt", [P, 2, PIX])
        res = sb("res", [P, 2, PIX])

        def bank(name, shape):
            return ctx.enter_context(nc.psum_tensor(name, shape, F32))

        kv_ps = [bank(f"kv_ps{u}", [128, BLOCKS, 2, HEADS, DIM]) for u in range(2)]
        q_ps = bank("q_ps", [128, 2, PIX])
        c_ps = bank("c_ps", [128, 512])
        o_ps = [bank(f"o_ps{u}", [128, 512]) for u in range(2)]
        MEAN, VAR = PIX, PIX + 1
        ctx_ps = c_ps[:, 0:2 * HIDDEN]
        fold_ps = c_ps[:, 2 * HIDDEN:2 * HIDDEN + 2 * CHANNELS]

        gavg_banks = (o_ps[0], o_ps[1], o_ps[1])

        x_in = [sem(f"x_in{n}") for n in range(len(LOADS))]
        par_in, mats_in, w_in, b_in = (sem(n) for n in ("par_in", "mats_in", "w_in", "b_in"))
        b_zero = sem("b_zero")
        ones_ready = sem("ones_ready")
        w_step = sem("w_step")
        w_ready = sem("w_ready")
        b_step = sem("b_step")
        b_ready = sem("b_ready")
        obc_done, obc_ready = sem("obc_done"), sem("obc_ready")
        xstat_ready, xmv_ready, gavg_done = sem("xstat_ready"), sem("xmv_ready"), sem("gavg_done")
        gn_step, pow_ready, rstd_ready = sem("gn_step"), sem("pow_ready"), sem("rstd_ready")
        coef_ready = sem("coef_ready")
        xn_ready, hi_ready, lo_ready = sem("xn_ready"), sem("hi_ready"), sem("lo_ready")
        xt_in = [sem(f"xt_in{u}") for u in range(2)]
        image1_done, kv_done, q_done = sem("image1_done"), sem("kv_done"), sem("q_done")
        kmax_ready, ksub_ready, kexp_ready = sem("kmax_ready"), sem("ksub_ready"), sem("kexp_ready")
        tree_step = sem("tree_step")
        ksum_ready, rks_ready, vs_ready = sem("ksum_ready"), sem("rks_ready"), sem("vs_ready")
        qmax_ready, qexp_ready, rq_ready = sem("qmax_ready"), sem("qexp_ready"), sem("rq_ready")
        ctx_done, ctxm_ready, fold_done, fold_ready = (
            sem("ctx_done"), sem("ctxm_ready"), sem("fold_done"), sem("fold_ready"))
        out_done, ostat_ready, omv_ready = sem("out_done"), sem("ostat_ready"), sem("omv_ready")
        cen_done, cdev_ready, msq_ready = sem("cen_done"), sem("cdev_ready"), sem("msq_ready")
        var_done, ve_ready, gn2_step, gn2_ready = (
            sem("var_done"), sem("ve_ready"), sem("gn2_step"), sem("gn2_ready"))
        tm_ready = sem("tm_ready")
        tt_ready, res_ready = sem("tt_ready"), sem("res_ready")
        stored = [sem(f"stored{u}") for u in range(2)]

        def at(j, u, lag):
            return 2 * j + u + lag, (u + lag) % 2, j + (u + lag) // 2

        def rows(image):
            return slice(image * CHANNELS, (image + 1) * CHANNELS)

        def there(p):
            return not isinstance(p, int) or 0 <= p < PAIRS

        def stacked(p):
            return not isinstance(p, int) or DIRECT <= p < PAIRS

        def wait(eng, semaphore, value):
            if not isinstance(value, int) or value > 0:
                eng.wait_ge(semaphore, value)

        def run_pipeline(eng, step, first, steady, last):
            a, b = steady if LOOPS else (last + 1, last + 1)
            for i in range(first, a):
                step(i // 2, i % 2)
            if b > a:
                with eng.Fori(a // 2, b // 2) as j:
                    for i in (a, a + 1):
                        step(j + (i // 2 - a // 2), i % 2)
            for i in range(b, last + 1):
                step(i // 2, i % 2)

        def group_of(p):
            return next(g for g, (a, b) in enumerate(NORMED) if p < b) if isinstance(p, int) else len(NORMED) - 1

        def of(tensor, p):
            return tensor[:, bass.ds(p, 1)]

        block = ctx.enter_context(nc.Block())

        @block.sync
        def _(sp):
            x_pair = x.rearrange("(p b) c n -> p (b c) n", b=2)
            o_pair = out.rearrange("(p b) c n -> p (b c) n", b=2)
            for n, (a, b) in enumerate(LOADS):
                sp.dma_start(x_sb[:, a:b, :], x_pair[a:b].rearrange("p c n -> c p n")).then_inc(x_in[n], DMA)

            def stack(j, u):
                p, r, h = at(j, u, 2)
                if not stacked(p):
                    return
                wait(sp, hi_ready, p - 1)
                wait(sp, q_done, p - 1)
                for part in range(2):
                    if part:
                        wait(sp, lo_ready, p - 1)
                    for image in range(2):
                        sp.dma_start(xt[rows(part), r, image, :].bitcast(F32),
                                     split[rows(image), r, part, :].bitcast(F32)).then_inc(xt_in[r], DMA)

            def store(j, u):
                p, r, h = at(j, u, -3)
                if not there(p):
                    return
                wait(sp, res_ready, p + 1)
                sp.dma_start(o_pair[p], res[:, r, :]).then_inc(stored[r], DMA)

            def step(j, u):
                stack(j, u)
                store(j, u)

            run_pipeline(sp, step, 0, (4, 6), PAIRS + 2)
            for u in range(2):
                sp.wait_ge(stored[u], DMA * PAIRS // 2)

        @block.gpsimd
        def _(pool):
            nc.gpsimd.memset(brow[:], 0.0).then_inc(b_zero, 1)
            nc.gpsimd.memset(minus_half[:], -0.5)
            nc.gpsimd.memset(ones[:].bitcast(F32), 1.0).then_inc(ones_ready, 1)

            def group_rstd(g):
                a, b = NORMED[g]
                pool.wait_ge(pow_ready, g + 1)
                nc.gpsimd.tensor_tensor(
                    rstd[:, a:b, :], pow_in[:, a:b, :],
                    minus_half[:, 2 * a:2 * b].rearrange("p (a t) -> p a t", t=2),
                    ALU.pow).then_inc(rstd_ready, 1)

            def low_part(j, u):
                p, r, h = at(j, u, 2)
                if not stacked(p):
                    return
                wait(pool, hi_ready, p - 1)
                nc.gpsimd.tensor_tensor(split[:, r, 1, :], xn[:, r, :], split[:, r, 0, :].bitcast(F32),
                                        ALU.subtract).then_inc(lo_ready, 1)

            def key_sums(j, u):
                p, r, h = at(j, u, 0)
                if not there(p):
                    return
                wait(pool, kexp_ready, p + 1)
                wait(pool, tree_step, 3 * p)
                e = ek[:, r, :].rearrange("p (g d) -> p g d", d=DIM)
                nc.gpsimd.tensor_tensor(tree[:], e[:, :, 0:8], e[:, :, 8:16], ALU.add).then_inc(tree_step, 1)
                pool.wait_ge(tree_step, 3 * p + 1)
                nc.gpsimd.tensor_tensor(tree2[:], tree[:, :, 0:4], tree[:, :, 4:8],
                                        ALU.add).then_inc(tree_step, 1)
                pool.wait_ge(tree_step, 3 * p + 2)
                wait(pool, ksum_ready, p)
                nc.gpsimd.tensor_tensor(tree3[:], tree2[:, :, 0:2], tree2[:, :, 2:4],
                                        ALU.add).then_inc(tree_step, 1)
                pool.wait_ge(tree_step, 3 * p + 3)
                wait(pool, rks_ready, p - 1)
                nc.gpsimd.tensor_tensor(ks[:, r, :], tree3[:, :, 0], tree3[:, :, 1],
                                        ALU.add).then_inc(ksum_ready, 1)

            def gn2_coefficients(j, u):
                p, r, h = at(j, u, -3)
                if not there(p):
                    return
                wait(pool, ve_ready, p + 1)
                wait(pool, tm_ready, p + 1)
                wait(pool, tt_ready, p - 1)
                nc.gpsimd.tensor_tensor(orstd[:, r:r + 1], ve[:, r:r + 1], minus_half[:, 0:1],
                                        ALU.pow).then_inc(gn2_step, 1)
                pool.wait_ge(gn2_step, 2 * p + 1)
                nc.gpsimd.tensor_tensor(coef_q[:, r:r + 1], orstd[:, r:r + 1], par[:, GN2_W:GN2_W + 1],
                                        ALU.mult).then_inc(gn2_step, 1)
                pool.wait_ge(gn2_step, 2 * p + 2)
                nc.gpsimd.tensor_scalar(coef_r[:, r:r + 1], tm[:, r:r + 1], coef_q[:, r:r + 1],
                                        of(rest0, p), ALU.mult, ALU.add).then_inc(gn2_ready, 1)

            def step(j, u):
                low_part(j, u)
                gn2_coefficients(j, u)
                key_sums(j, u)

            pool.wait_ge(par_in, DMA)
            pool.wait_ge(ones_ready, 1)
            group_rstd(0)
            group_rstd(1)
            pool.wait_ge(w_step, 2)
            nc.gpsimd.tensor_tensor(w_lo[:], w_f, w_hi[:].bitcast(F32), ALU.subtract).then_inc(w_ready, 1)
            step(0, 0)
            group_rstd(2)
            run_pipeline(pool, step, 1, (4, 6), PAIRS + 2)

        @block.scalar
        def _(act):
            act.dma_start(par_avg[:], params).then_inc(par_in, DMA)
            act.dma_start(w_all[:], weights).then_inc(w_in, DMA)
            act.wait_ge(b_zero, 1)
            act.dma_start(brow[0:33:32, :], b_qkv).then_inc(b_in, DMA)
            act.dma_start(mats[:], matrices).then_inc(mats_in, DMA)
            act.preload_act_table(ACT.Exp)

            def split_weights():
                act.wait_ge(w_step, 1)
                nc.scalar.activation(w_hi[:], w_f[:], ACT.Copy).then_inc(w_step, 1)

            def affine(j, u):
                p, r, h = at(j, u, 3)
                if not there(p):
                    return
                wait(act, coef_ready, group_of(p) + 1)
                if stacked(p - 2):
                    wait(act, lo_ready, p - 3)
                else:
                    wait(act, q_done, p - 1)
                nc.scalar.activation(xn[:, r, :], x_sb[:, p, :], ACT.Identity, bias=of(coef_b, p),
                                     scale=of(coef_a, p)).then_inc(xn_ready, 1)

            def high_part(j, u):
                p, r, h = at(j, u, 3)
                if not stacked(p):
                    return
                wait(act, xn_ready, p + 1)
                wait(act, xt_in[r], 4 * DMA * (h - 1))
                nc.scalar.activation(split[:, r, 0, :], xn[:, r, :], ACT.Copy).then_inc(hi_ready, 1)

            def key_exp(j, u):
                p, r, h = at(j, u, 0)
                if not there(p):
                    return
                wait(act, ksub_ready, p + 1)
                nc.scalar.activation(ek[:, r, :], ek[:, r, :], ACT.Exp).then_inc(kexp_ready, 1)

            def query_exp(j, u):
                p, r, h = at(j, u, 0)
                if not there(p):
                    return
                wait(act, qmax_ready, p + 1)
                wait(act, out_done, p - 1)
                wait(act, rq_ready, p - 1)
                for image in range(2):
                    last = nc.scalar.activation(eq[:, r, image, :], q_ps[:, image, :], ACT.Exp,
                                                bias=nqmax[:, r, image:image + 1],
                                                accum_out=qs[:, r, image:image + 1])
                last.then_inc(qexp_ready, 1)

            def fold_copy(j, u):
                p, r, h = at(j, u, -1)
                if not there(p):
                    return
                wait(act, fold_done, p + 1)
                wait(act, rq_ready, p + 1)
                wait(act, out_done, p - 1)
                for image in range(2):
                    last = nc.scalar.activation(fold[:, r, image, :],
                                                fold_ps[:, image * CHANNELS:(image + 1) * CHANNELS],
                                                ACT.Copy, scale=rq[:, r, image:image + 1])
                last.then_inc(fold_ready, 1)

            def normalise(j, u):
                p, r, h = at(j, u, -3)
                if not there(p):
                    return
                wait(act, gn2_ready, p + 1)
                wait(act, res_ready, p - 1)
                nc.scalar.activation(tt[:, r, :], o_ps[r][:, 0:PIX], ACT.Identity,
                                     bias=coef_r[:, r:r + 1], scale=coef_q[:, r:r + 1]).then_inc(tt_ready, 1)

            def step(j, u):
                key_exp(j, u)
                normalise(j, u)
                query_exp(j, u)
                fold_copy(j, u)
                affine(j, u)
                high_part(j, u)

            affine(-2, 1)
            split_weights()
            affine(-1, 0)
            affine(-1, 1)
            high_part(-1, 1)
            step(0, 0)
            run_pipeline(act, step, 1, (4, 6), PAIRS + 2)

        @block.tensor
        def _(pe):
            def warm_up(count):
                for n in range(count):
                    nc.tensor.matmul(kv_ps[1][:, 0:2, :, :, :], ones[:, 0:128], ones[:], start=True,
                                     stop=True)

            def group_average(g):
                a, b = NORMED[g]
                pe.wait_ge(xmv_ready, g + 1)
                wait(pe, coef_ready, g if g == 2 else 0)
                nc.tensor.matmul(gavg_banks[g][:, 0:2 * (b - a)], avg_group,
                                 xmv[:, a:b, :], start=True, stop=True).then_inc(gavg_done, 1)

            def keys_values(j, u):
                p, r, h = at(j, u, 1)
                if not stacked(p):
                    return
                wait(pe, xt_in[r], 4 * DMA * (h)   )
                wait(pe, vs_ready, p - 1)
                for image in range(2):
                    for chunk in range(CHUNKS):
                        nc.tensor.matmul(kv_ps[r][:, image * CHUNKS + chunk, :, :, :], ones[:, 0:128],
                                         bsplit[:, HIDDEN:3 * HIDDEN], start=(chunk == 0), stop=False,
                                         skip_group_check=True)
                    for chunk in range(CHUNKS):
                        pixels = xt[:, r, image, chunk * 128:(chunk + 1) * 128]
                        for w in (w_hi, w_lo):
                            ins = nc.tensor.matmul(kv_ps[r][:, image * CHUNKS + chunk, :, :, :], pixels,
                                                   w[:, HIDDEN:3 * HIDDEN], start=False,
                                                   stop=(chunk == CHUNKS - 1 and w is w_lo),
                                                   skip_group_check=True)
                ins.then_inc(kv_done, 1)

            def queries(j, u):
                p, r, h = at(j, u, 1)
                if not stacked(p):
                    return
                wait(pe, xt_in[r], 4 * DMA * (h)   )
                wait(pe, qexp_ready, p)
                nc.tensor.matmul(q_ps[:, :, :], bsplit[:, 0:HIDDEN],
                                 ones[:].rearrange("p (i n) -> p i n", i=2), start=True, stop=False,
                                 skip_group_check=True)
                for w in (w_hi, w_lo):
                    ins = nc.tensor.matmul(q_ps[:, :, :], w[:, 0:HIDDEN], xt[:, r, :, :], start=False,
                                           stop=(w is w_lo), skip_group_check=True)
                ins.then_inc(q_done, 1)

            def context(j, u):
                p, r, h = at(j, u, -1)
                if not there(p):
                    return
                wait(pe, vs_ready, p + 1)
                wait(pe, fold_ready, p)
                for blk in range(BLOCKS):
                    image, chunk = divmod(blk, CHUNKS)
                    cols = slice(blk * HIDDEN, (blk + 1) * HIDDEN)
                    ins = nc.tensor.matmul(ctx_ps[:, image * HIDDEN:(image + 1) * HIDDEN],
                                           vs[:, r, cols], ek[:, r, cols],
                                           start=(blk == 0), stop=(chunk == CHUNKS - 1), skip_group_check=True)
                ins.then_inc(ctx_done, 1)

            def folds(j, u):
                p, r, h = at(j, u, -1)
                if not there(p):
                    return
                wait(pe, ctxm_ready, p + 1)
                for image in range(2):
                    ins = nc.tensor.matmul(fold_ps[:, image * CHANNELS:(image + 1) * CHANNELS],
                                           ctxm[:, image, :], wo_sb[:], start=False, stop=True,
                                           skip_group_check=True)
                ins.then_inc(fold_done, 1)

            def outputs(j, u):
                p, r, h = at(j, u, -2)
                if not there(p):
                    return
                wait(pe, fold_ready, p + 1)
                wait(pe, tt_ready, p - 1)
                for image in range(2):
                    ins = nc.tensor.matmul(o_ps[r][image * CHANNELS:(image + 1) * CHANNELS, 0:PIX],
                                           fold[:, r, image, :], eq[:, r, image, :], start=True, stop=True)
                ins.then_inc(out_done, 1)

            def centre(j, u):
                p, r, h = at(j, u, -2)
                if not there(p):
                    return
                wait(pe, omv_ready, p + 1)
                nc.tensor.matmul(o_ps[r][:, MEAN:MEAN + 1], mats[:, CENTER, :], omv[:, r, 0:1],
                                 start=True, stop=True).then_inc(cen_done, 1)

            def variance(j, u):
                p, r, h = at(j, u, -3)
                if not there(p):
                    return
                wait(pe, msq_ready, p + 1)
                nc.tensor.matmul(o_ps[r][:, VAR:VAR + 1], mats[:, AVG_IMAGE, :], msq[:, r:r + 1],
                                 start=True, stop=True).then_inc(var_done, 1)

            def step(j, u):
                outputs(j, u)
                variance(j, u)
                context(j, u)
                keys_values(j, u)
                folds(j, u)
                centre(j, u)
                queries(j, u)

            def direct_keys_values(p):
                pe.wait_ge(xn_ready, p + 1)
                pe.wait_ge(w_step, 1)
                for image in (1, 0):
                    for chunk in range(CHUNKS):
                        ins = nc.tensor.matmul(kv_ps[p][:, image * CHUNKS + chunk, :, :, :],
                                               xn[rows(image), p, chunk * 128:(chunk + 1) * 128],
                                               w_f[rows(image), HIDDEN:3 * HIDDEN], start=(chunk == 0),
                                               stop=False, skip_group_check=True)
                    if image == 1:
                        ins.then_inc(image1_done, 1)
                pe.wait_ge(b_ready, 1)
                for blk in range(BLOCKS):
                    if blk == CHUNKS:
                        pe.wait_ge(image1_done, 2 * p + 1)
                    ins = nc.tensor.matmul(kv_ps[p][:, blk, :, :, :], ones[:, 0:128],
                                           bsplit[:, HIDDEN:3 * HIDDEN], start=False,
                                           stop=(blk % CHUNKS == CHUNKS - 1), skip_group_check=True)
                ins.then_inc(kv_done, 1)

            def direct_queries(p):
                wait(pe, qexp_ready, p)
                nc.tensor.matmul(q_ps[:, 1, :], w_f[rows(1), 0:HIDDEN], xn[rows(1), p, :],
                                 start=True, stop=False, skip_group_check=True).then_inc(image1_done, 1)
                pe.wait_ge(image1_done, 2 * p + 2)
                nc.tensor.matmul(q_ps[:, 0, :], w_f[rows(0), 0:HIDDEN], xn[rows(0), p, :],
                                 start=False, stop=False, skip_group_check=True)
                nc.tensor.matmul(q_ps[:, :, :], bsplit[:, 0:HIDDEN],
                                 ones[:].rearrange("p (i n) -> p i n", i=2), start=False, stop=True,
                                 skip_group_check=True).then_inc(q_done, 1)

            pe.wait_ge(ones_ready, 1)
            warm_up(WARM[0])
            pe.wait_ge(par_in, DMA)
            group_average(0)
            warm_up(WARM[1])
            group_average(1)
            warm_up(WARM[2])
            direct_keys_values(0)
            direct_queries(0)
            direct_keys_values(1)
            group_average(2)
            pe.wait_ge(mats_in, DMA)
            pe.wait_ge(coef_ready, 1)
            nc.tensor.matmul(o_ps[0][:, 0:1], mats[:, CENTER, :], par[:, OUT_B:OUT_B + 1],
                             start=True, stop=True).then_inc(obc_done, 1)
            direct_queries(1)
            pe.wait_ge(w_ready, 1)
            step(0, 1)
            pe.wait_ge(coef_ready, len(NORMED))
            pe.wait_ge(obc_ready, 1)
            run_pipeline(pe, step, 2, (3, 7), PAIRS + 2)

        @block.vector
        def _(dve):
            def channel_stats(g):
                a, b = NORMED[g]
                for n, (first, last) in enumerate(LOADS):
                    for p in range(max(a, first), min(b, last)):
                        dve.wait_ge(x_in[n], DMA)
                        nc.vector.bn_stats(xstat[:, p, :], x_sb[:, p, :]).then_inc(xstat_ready, 1)
                for p in range(a, b):
                    dve.wait_ge(xstat_ready, p + 1)
                    ins = nc.vector.bn_aggr(xmv[:, p, :], xstat[:, p, :])
                ins.then_inc(xmv_ready, 1)

            def group_variance(g):
                a, b = NORMED[g]
                avg = gavg_banks[g][:, 0:2 * (b - a)].rearrange("p (a t) -> p a t", t=2)
                s = GN_STEPS * g
                dve.wait_ge(gavg_done, g + 1)
                nc.vector.tensor_tensor(dev[:, a:b], xmv[:, a:b, 0], avg[:, :, 0],
                                        ALU.subtract).then_inc(gn_step, 1)
                dve.wait_ge(gn_step, s + 1)
                nc.vector.tensor_tensor(dev2[:, a:b], dev[:, a:b], dev[:, a:b], ALU.mult).then_inc(gn_step, 1)
                dve.wait_ge(gn_step, s + 2)
                nc.vector.tensor_tensor(gvar[:, a:b], dev2[:, a:b], avg[:, :, 1], ALU.add).then_inc(gn_step, 1)
                dve.wait_ge(gn_step, s + 3)
                nc.vector.tensor_scalar(pow_in[:, a:b, 0], gvar[:, a:b], EPS, None, ALU.add)
                nc.vector.tensor_scalar(pow_in[:, a:b, 1], gvar[:, a:b], 1.0 + EPS, EPS * EPS,
                                        ALU.mult, ALU.add).then_inc(pow_ready, 1)

            def group_coefficients(g):
                a, b = NORMED[g]
                avg = gavg_banks[g][:, 0:2 * (b - a)].rearrange("p (a t) -> p a t", t=2)
                s = GN_STEPS * g
                dve.wait_ge(rstd_ready, g + 1)
                dve.wait_ge(par_in, DMA)
                nc.vector.tensor_scalar(coef_a[:, a:b], rstd[:, a:b, 1], par[:, GN1_W:GN1_W + 1], None,
                                        ALU.mult).then_inc(gn_step, 1)
                nc.vector.tensor_scalar(coef_p[:, a:b], rstd[:, a:b, 0], 1.0, None, ALU.add)
                nc.vector.tensor_tensor(mean_r[:, a:b], rstd[:, a:b, 0], avg[:, :, 0],
                                        ALU.mult).then_inc(gn_step, 1)
                dve.wait_ge(gn_step, s + 5)
                nc.vector.tensor_tensor(mean_a[:, a:b], coef_a[:, a:b], avg[:, :, 0],
                                        ALU.mult).then_inc(gn_step, 1)
                nc.vector.tensor_scalar(rest0[:, a:b], mean_r[:, a:b], -1.0, par[:, GN2_B:GN2_B + 1],
                                        ALU.mult, ALU.add)
                dve.wait_ge(gn_step, s + 6)
                nc.vector.tensor_scalar(coef_b[:, a:b], mean_a[:, a:b], -1.0, par[:, GN1_B:GN1_B + 1],
                                        ALU.mult, ALU.add).then_inc(coef_ready, 1)

            def prepare_weights():
                dve.wait_ge(w_in, DMA)
                nc.vector.tensor_scalar(w_f[:, 0:HIDDEN], w_f[:, 0:HIDDEN], QSCALE, None,
                                        ALU.mult).then_inc(w_step, 1)

            def prepare_bias():
                dve.wait_ge(b_in, DMA)
                nc.vector.tensor_scalar(brow[:, 0:HIDDEN], brow[:, 0:HIDDEN], QSCALE, None,
                                        ALU.mult).then_inc(b_step, 1)
                dve.wait_ge(b_step, 1)
                nc.vector.tensor_copy(bsplit[:], brow[:]).then_inc(b_step, 1)
                dve.wait_ge(b_step, 2)
                nc.vector.tensor_tensor(bsplit[32:33, :], brow[32:33, :], bsplit[32:33, :].bitcast(F32),
                                        ALU.subtract).then_inc(b_ready, 1)

            def keys_of(r):
                return kv_ps[r][:, :, 0, :, :]

            def values_of(r):
                return kv_ps[r][:, :, 1, :, :]

            def per_head(t):
                return t.rearrange("p (b g d) -> p b g d", b=BLOCKS, g=HEADS)

            def spread(t):
                return t.rearrange("p (b g) -> p b g", b=BLOCKS).unsqueeze(3).broadcast_to(
                    [128, BLOCKS, HEADS, DIM])

            def key_max(j, u):
                p, r, h = at(j, u, 0)
                if not there(p):
                    return
                wait(dve, kv_done, p + 1)
                wait(dve, ksub_ready, p)
                nc.vector.tensor_reduce(kmx[:], keys_of(r), AX.X, ALU.max).then_inc(kmax_ready, 1)

            def key_shift(j, u):
                p, r, h = at(j, u, 0)
                if not there(p):
                    return
                wait(dve, kmax_ready, p + 1)
                wait(dve, ctx_done, p - 1)
                nc.vector.tensor_tensor(per_head(ek[:, r, :]), keys_of(r), spread(kmx[:]),
                                        ALU.subtract).then_inc(ksub_ready, 1)

            def query_max(j, u):
                p, r, h = at(j, u, 0)
                if not there(p):
                    return
                wait(dve, q_done, p + 1)
                nc.vector.tensor_reduce(nqmax[:, r, :], q_ps[:, :, :], AX.X, ALU.max,
                                        negate=True).then_inc(qmax_ready, 1)

            def key_norm(j, u):
                p, r, h = at(j, u, -1)
                if not there(p):
                    return
                wait(dve, ksum_ready, p + 1)
                wait(dve, vs_ready, p)
                nc.vector.reciprocal(rks[:], ks[:, r, :]).then_inc(rks_ready, 1)

            def scale_values(j, u):
                p, r, h = at(j, u, -1)
                if not there(p):
                    return
                wait(dve, rks_ready, p + 1)
                wait(dve, ctx_done, p - 1)
                nc.vector.tensor_tensor(per_head(vs[:, r, :]), values_of(r), spread(rks[:]),
                                        ALU.mult).then_inc(vs_ready, 1)

            def mask_context(j, u):
                p, r, h = at(j, u, -1)
                if not there(p):
                    return
                wait(dve, qexp_ready, p + 1)
                wait(dve, fold_ready, p - 1)
                nc.vector.reciprocal(rq[:, r, :], qs[:, r, :]).then_inc(rq_ready, 1)
                wait(dve, ctx_done, p + 1)
                wait(dve, fold_done, p)
                nc.vector.tensor_tensor(ctxm[:], ctx_ps.rearrange("p (i d) -> p i d", i=2),
                                        mats[:, HEAD_MASK, :].unsqueeze(1).broadcast_to([P, 2, HIDDEN]),
                                        ALU.mult).then_inc(ctxm_ready, 1)

            def output_stats(j, u):
                p, r, h = at(j, u, -2)
                if not there(p):
                    return
                wait(dve, out_done, p + 1)
                wait(dve, omv_ready, p)
                nc.vector.bn_stats(ostat[:], o_ps[r][:, 0:PIX]).then_inc(ostat_ready, 1)

            def output_moments_waits(j, u):
                p, r, h = at(j, u, -2)
                if not there(p):
                    return
                wait(dve, ostat_ready, p + 1)
                wait(dve, tm_ready, p - 1)

            def output_moments(j, u):
                p, r, h = at(j, u, -2)
                if not there(p):
                    return
                nc.vector.bn_aggr(omv[:, r, :], ostat[:]).then_inc(omv_ready, 1)

            def deviation(j, u):
                p, r, h = at(j, u, -3)
                if not there(p):
                    return
                wait(dve, obc_ready, 1)
                wait(dve, cen_done, p + 1)
                nc.vector.tensor_tensor(cdev[:, r:r + 1], o_ps[r][:, MEAN:MEAN + 1], obc[:],
                                        ALU.add).then_inc(cdev_ready, 1)

            def squared_deviation(j, u):
                p, r, h = at(j, u, -3)
                if not there(p):
                    return
                wait(dve, cdev_ready, p + 1)
                nc.vector.scalar_tensor_tensor(out=msq[:, r:r + 1], in0=cdev[:, r:r + 1],
                                               scalar=cdev[:, r:r + 1], in1=omv[:, r, 1:2],
                                               op0=ALU.mult, op1=ALU.add).then_inc(msq_ready, 1)
                nc.vector.tensor_tensor(tm[:, r:r + 1], cdev[:, r:r + 1], omv[:, r, 0:1],
                                        ALU.subtract).then_inc(tm_ready, 1)

            def variance_eps(j, u):
                p, r, h = at(j, u, -3)
                if not there(p):
                    return
                wait(dve, var_done, p + 1)
                nc.vector.tensor_scalar(ve[:, r:r + 1], o_ps[r][:, VAR:VAR + 1], EPS, None, ALU.add).then_inc(ve_ready, 1)

            def finish(j, u):
                p, r, h = at(j, u, -3)
                if not there(p):
                    return
                wait(dve, tt_ready, p + 1)
                wait(dve, stored[r], DMA * h)
                nc.vector.scalar_tensor_tensor(out=res[:, r, :], in0=x_sb[:, p, :], scalar=of(coef_p, p),
                                               in1=tt[:, r, :], op0=ALU.mult,
                                               op1=ALU.add).then_inc(res_ready, 1)

            def step(j, u):
                key_max(j, u)
                deviation(j, u)
                key_norm(j, u)
                squared_deviation(j, u)
                scale_values(j, u)
                variance_eps(j, u)
                key_shift(j, u)
                query_max(j, u)
                mask_context(j, u)
                output_stats(j, u)
                output_moments_waits(j, u)
                finish(j, u)
                output_moments(j, u)

            channel_stats(0)
            group_variance(0)
            prepare_weights()
            channel_stats(1)
            group_coefficients(0)
            group_variance(1)
            prepare_bias()
            group_coefficients(1)
            channel_stats(2)
            step(0, 0)
            group_variance(2)
            dve.wait_ge(obc_done, 1)
            nc.vector.tensor_copy(obc[:], o_ps[0][:, 0:1]).then_inc(obc_ready, 1)
            step(0, 1)
            group_coefficients(2)
            run_pipeline(dve, step, 2, (4, 8), PAIRS + 2)


GN_STEPS = 6
LOOPS = True
WARM = (5, 5, 4)


def kernel(**inputs):
    import concourse.bacc as bacc
    from concourse.bass_utils import run_bass_kernel_spmd

    arr = {k: np.ascontiguousarray(v) for k, v in inputs.items()}
    names = ("gn1_w", "gn1_b", "out_b", "gn2_w", "gn2_b")
    params = np.stack([np.concatenate([arr["L0_conv_" + n]] * 2) for n in names], axis=1)
    c = np.arange(P)
    group = (c[:, None] // GROUP_CH == c[None, :] // GROUP_CH) / GROUP_CH
    image = (c[:, None] // CHANNELS == c[None, :] // CHANNELS) / CHANNELS
    heads = c[:, None] // DIM == c[None, :] // DIM
    matrices = np.stack([np.eye(P) - image, image, heads], axis=1).astype(np.float32)
    data = {
        "x": arr["x"].reshape(IMAGES, CHANNELS, PIX),
        "params": np.concatenate([params, group.astype(np.float32)], axis=1),
        "weights": np.concatenate([np.concatenate([arr["L0_conv_qkv_w"].T] * 2), arr["L0_conv_out_w"].T], axis=1),
        "b_qkv": np.stack([arr["L0_conv_qkv_b"]] * 2),
        "matrices": matrices,
    }
    nc = bacc.Bacc("TRN2", target_bir_lowering=False, num_devices=1)
    args = [nc.dram_tensor(n + "_dram", a.shape, mybir.dt.from_np(a.dtype), kind="ExternalInput").ap()
            for n, a in data.items()]
    out = nc.dram_tensor("out_dram", (IMAGES, CHANNELS, PIX), F32, kind="ExternalOutput").ap()
    attention_kernel(nc, *args, out)
    r = run_bass_kernel_spmd(nc, [{n + "_dram": a for n, a in data.items()}], core_ids=[0])
    return r.results[0]["out_dram"].reshape(IMAGES, CHANNELS, SIDE, SIDE)
```

```python
import numpy as np
import concourse.bass as bass
import concourse.mybir as mybir
from contextlib import ExitStack

F32 = mybir.dt.float32
F32R = mybir.dt.float32r
ALU = mybir.AluOpType
ACT = mybir.ActivationFunctionType
AX = mybir.AxisListType

IMAGES, CHANNELS, SIDE = 16, 64, 16
PIX = SIDE * SIDE
HEADS, DIM = 8, 16
HIDDEN = HEADS * DIM
PAIRS = IMAGES // 2
P = 2 * CHANNELS
CHUNKS = PIX // 128
BLOCKS = 2 * CHUNKS
GROUPS = 32
GROUP_CH = CHANNELS // GROUPS
EPS = 1e-5
QSCALE = DIM ** -0.5
GROUPED = ((0, 1), (1, 3), (3, 5), (5, 8))
DIRECT = 2
DMA = 16

GN1_W, GN1_B, OUT_B, GN2_W, GN2_B, PARAMS = range(6)
CENTER, AVG_IMAGE, HEAD_MASK, MATRICES = range(4)


def attention_kernel(nc, x, params, weights, b_qkv, matrices, out):
    ctx = ExitStack()
    with ctx:
        def sb(name, shape, dt=F32):
            return ctx.enter_context(nc.sbuf_tensor(name, shape, dt))

        def sem(name):
            return ctx.enter_context(nc.semaphore(name))

        x_sb = sb("x_sb", [P, PAIRS, PIX])
        par_avg = sb("par_avg", [P, PARAMS + P])
        par, avg_group = par_avg[:, 0:PARAMS], par_avg[:, PARAMS:PARAMS + P]
        mats = sb("mats", [P, MATRICES, P])
        w_all = sb("w_all", [P, 3 * HIDDEN + CHANNELS])
        w_f, wo_sb = w_all[:, 0:3 * HIDDEN], w_all[:, 3 * HIDDEN:]
        w_hi = sb("w_hi", [P, 3 * HIDDEN], F32R)
        w_lo = sb("w_lo", [P, 3 * HIDDEN], F32R)
        brow = sb("brow", [P, 3 * HIDDEN])
        bsplit = sb("bsplit", [P, 3 * HIDDEN], F32R)
        ones = sb("ones", [P, 512], F32R)
        xstat = sb("xstat", [P, PAIRS, 6])
        xmv = sb("xmv", [P, PAIRS, 2])
        dev = sb("dev", [P, PAIRS])
        dev2 = sb("dev2", [P, PAIRS])
        gvar = sb("gvar", [P, PAIRS])
        pow_in = sb("pow_in", [P, PAIRS, 2])
        rstd = sb("rstd", [P, PAIRS, 2])
        minus_half = sb("minus_half", [P, 2 * PAIRS])
        coef_a = sb("coef_a", [P, PAIRS])
        mean_a = sb("mean_a", [P, PAIRS])
        coef_b = sb("coef_b", [P, PAIRS])
        coef_p = sb("coef_p", [P, PAIRS])
        mean_r = sb("mean_r", [P, PAIRS])
        rest0 = sb("rest0", [P, PAIRS])
        xn = sb("xn", [P, 2, PIX])
        split = sb("split", [P, 2, 2, PIX], F32R)
        xt = sb("xt", [P, 2, 2, PIX], F32R)
        kmx = sb("kmx", [128, BLOCKS * HEADS])
        ek = sb("ek", [128, 2, BLOCKS * HIDDEN])
        tree = sb("tree", [128, BLOCKS * HEADS, 8])
        tree2 = sb("tree2", [128, BLOCKS * HEADS, 4])
        tree3 = sb("tree3", [128, BLOCKS * HEADS, 2])
        ks = sb("ks", [128, 2, BLOCKS * HEADS])
        rks = sb("rks", [128, BLOCKS * HEADS])
        vs = sb("vs", [128, 2, BLOCKS * HIDDEN])
        nqmax = sb("nqmax", [HIDDEN, 2, 2])
        eq = sb("eq", [HIDDEN, 2, 2, PIX])
        qs = sb("qs", [HIDDEN, 2, 2])
        rq = sb("rq", [HIDDEN, 2, 2])
        ctxm = sb("ctxm", [HIDDEN, 2, HIDDEN])
        fold = sb("fold", [HIDDEN, 2, 2, CHANNELS])
        ostat = sb("ostat", [P, 6])
        omv = sb("omv", [P, 2, 2])
        cdev = sb("cdev", [P, 2])
        msq = sb("msq", [P, 2])
        ve = sb("ve", [P, 2])
        orstd = sb("orstd", [P, 2])
        obc = sb("obc", [P, 1])
        tm = sb("tm", [P, 2])
        tt = sb("tt", [P, 2, PIX])
        skip = sb("skip", [P, PAIRS, PIX])
        res = sb("res", [P, PAIRS, PIX])

        def bank(name, shape):
            return ctx.enter_context(nc.psum_tensor(name, shape, F32))

        kv_ps = [bank(f"kv_ps{u}", [128, BLOCKS, 2, HEADS, DIM]) for u in range(2)]
        q_ps = bank("q_ps", [128, 2, PIX])
        c_ps = bank("c_ps", [128, 512])
        o_ps = [bank(f"o_ps{u}", [128, 512]) for u in range(2)]
        MEAN, VAR = PIX, PIX + 1
        ctx_ps = c_ps[:, 0:2 * HIDDEN]
        fold_ps = c_ps[:, 2 * HIDDEN:2 * HIDDEN + 2 * CHANNELS]

        gavg_banks = (o_ps[0], o_ps[1]) * 2

        x_in = [sem(f"x_in{n}") for n in range(len(GROUPED))]
        par_in, mats_in, w_in, b_in = (sem(n) for n in ("par_in", "mats_in", "w_in", "b_in"))
        b_zero = sem("b_zero")
        ones_ready = sem("ones_ready")
        w_step = sem("w_step")
        w_ready = sem("w_ready")
        b_step = sem("b_step")
        b_ready = sem("b_ready")
        obc_done, obc_ready = sem("obc_done"), sem("obc_ready")
        xstat_ready, xmv_ready, gavg_done = sem("xstat_ready"), sem("xmv_ready"), sem("gavg_done")
        gn_step, pow_ready, rstd_ready = sem("gn_step"), sem("pow_ready"), sem("rstd_ready")
        coef_ready = sem("coef_ready")
        xn_ready, hi_ready, lo_ready = sem("xn_ready"), sem("hi_ready"), sem("lo_ready")
        xt_in = [sem(f"xt_in{u}") for u in range(2)]
        image1_done, kv_done, q_done = sem("image1_done"), sem("kv_done"), sem("q_done")
        kmax_ready, ksub_ready, kexp_ready = sem("kmax_ready"), sem("ksub_ready"), sem("kexp_ready")
        tree_step = sem("tree_step")
        ksum_ready, rks_ready, vs_ready = sem("ksum_ready"), sem("rks_ready"), sem("vs_ready")
        qmax_ready, qexp_ready, rq_ready = sem("qmax_ready"), sem("qexp_ready"), sem("rq_ready")
        ctx_done, ctxm_ready, fold_done, fold_ready = (
            sem("ctx_done"), sem("ctxm_ready"), sem("fold_done"), sem("fold_ready"))
        out_done, ostat_ready, omv_ready = sem("out_done"), sem("ostat_ready"), sem("omv_ready")
        cen_done, cdev_ready, msq_ready = sem("cen_done"), sem("cdev_ready"), sem("msq_ready")
        var_done, ve_ready, gn2_ready = sem("var_done"), sem("ve_ready"), sem("gn2_ready")
        tm_ready = sem("tm_ready")
        tt_ready, res_ready = sem("tt_ready"), sem("res_ready")
        stored = sem("stored")

        def at(j, u, lag):
            return 2 * j + u + lag, (u + lag) % 2, j + (u + lag) // 2

        def rows(image):
            return slice(image * CHANNELS, (image + 1) * CHANNELS)

        def there(p):
            return not isinstance(p, int) or 0 <= p < PAIRS

        def stacked(p):
            return not isinstance(p, int) or DIRECT <= p < PAIRS

        def wait(eng, semaphore, value):
            if not isinstance(value, int) or value > 0:
                eng.wait_ge(semaphore, value)

        def run_pipeline(eng, step, first, steady, last):
            a, b = steady
            for i in range(first, a):
                step(i // 2, i % 2)
            with eng.Fori(a // 2, b // 2) as j:
                for i in (a, a + 1):
                    step(j + (i // 2 - a // 2), i % 2)
            for i in range(b, last + 1):
                step(i // 2, i % 2)

        def group_of(p):
            return next(g for g, (a, b) in enumerate(GROUPED) if p < b) if isinstance(p, int) else len(GROUPED) - 1

        def of(tensor, p):
            return tensor[:, bass.ds(p, 1)]

        block = ctx.enter_context(nc.Block())

        @block.sync
        def _(sp):
            x_pair = x.rearrange("(p b) c n -> p (b c) n", b=2)
            o_pair = out.rearrange("(p b) c n -> p (b c) n", b=2)
            for n, (a, b) in enumerate(GROUPED):
                sp.dma_start(x_sb[:, a:b, :], x_pair[a:b].rearrange("p c n -> c p n")).then_inc(x_in[n], DMA)

            def stack(j, u):
                p, r, h = at(j, u, 2)
                if not stacked(p):
                    return
                wait(sp, hi_ready, p - 1)
                wait(sp, q_done, p - 1)
                for part in range(2):
                    if part:
                        wait(sp, lo_ready, p - 1)
                    for image in range(2):
                        sp.dma_start(xt[rows(part), r, image, :].bitcast(F32),
                                     split[rows(image), r, part, :].bitcast(F32)).then_inc(xt_in[r], DMA)

            def store(j, u):
                p, r, h = at(j, u, -3)
                if not there(p):
                    return
                wait(sp, res_ready, p + 1)
                sp.dma_start(o_pair[p], res[:, p, :]).then_inc(stored, DMA)

            def step(j, u):
                stack(j, u)
                store(j, u)

            run_pipeline(sp, step, 0, (4, 6), PAIRS + 2)
            sp.wait_ge(stored, DMA * PAIRS)

        @block.gpsimd
        def _(pool):
            nc.gpsimd.memset(brow[:], 0.0).then_inc(b_zero, 1)
            nc.gpsimd.memset(minus_half[:], -0.5)
            nc.gpsimd.memset(ones[:].bitcast(F32), 1.0).then_inc(ones_ready, 1)

            def group_rstd(g):
                a, b = GROUPED[g]
                pool.wait_ge(pow_ready, g + 1)
                nc.gpsimd.tensor_tensor(
                    rstd[:, a:b, :], pow_in[:, a:b, :],
                    minus_half[:, 2 * a:2 * b].rearrange("p (a t) -> p a t", t=2),
                    ALU.pow).then_inc(rstd_ready, 1)

            def low_part(j, u):
                p, r, h = at(j, u, 2)
                if not stacked(p):
                    return
                wait(pool, hi_ready, p - 1)
                nc.gpsimd.tensor_tensor(split[:, r, 1, :], xn[:, r, :], split[:, r, 0, :].bitcast(F32),
                                        ALU.subtract).then_inc(lo_ready, 1)

            def key_sums(j, u):
                p, r, h = at(j, u, 0)
                if not there(p) or (isinstance(p, int) and p == PAIRS - 1):
                    return
                wait(pool, kexp_ready, p + 1)
                wait(pool, tree_step, 3 * p)
                e = ek[:, r, :].rearrange("p (g d) -> p g d", d=DIM)
                nc.gpsimd.tensor_tensor(tree[:], e[:, :, 0:8], e[:, :, 8:16], ALU.add).then_inc(tree_step, 1)
                pool.wait_ge(tree_step, 3 * p + 1)
                nc.gpsimd.tensor_tensor(tree2[:], tree[:, :, 0:4], tree[:, :, 4:8],
                                        ALU.add).then_inc(tree_step, 1)
                pool.wait_ge(tree_step, 3 * p + 2)
                wait(pool, ksum_ready, p)
                nc.gpsimd.tensor_tensor(tree3[:], tree2[:, :, 0:2], tree2[:, :, 2:4],
                                        ALU.add).then_inc(tree_step, 1)
                pool.wait_ge(tree_step, 3 * p + 3)
                wait(pool, rks_ready, p - 1)
                nc.gpsimd.tensor_tensor(ks[:, r, :], tree3[:, :, 0], tree3[:, :, 1],
                                        ALU.add).then_inc(ksum_ready, 1)

            def gn2_scale(j, u):
                p, r, h = at(j, u, -3)
                if not there(p):
                    return
                wait(pool, ve_ready, p + 1)
                nc.gpsimd.tensor_tensor(orstd[:, r:r + 1], ve[:, r:r + 1], minus_half[:, 0:1],
                                        ALU.pow).then_inc(gn2_ready, 1)

            def step(j, u):
                low_part(j, u)
                gn2_scale(j, u)
                key_sums(j, u)

            pool.wait_ge(par_in, DMA)
            pool.wait_ge(ones_ready, 1)
            group_rstd(0)
            group_rstd(1)
            pool.wait_ge(w_step, 2)
            nc.gpsimd.tensor_tensor(w_lo[:], w_f, w_hi[:].bitcast(F32), ALU.subtract).then_inc(w_ready, 1)
            group_rstd(2)
            step(0, 0)
            group_rstd(3)
            run_pipeline(pool, step, 1, (4, 6), PAIRS + 2)

        @block.scalar
        def _(act):
            act.dma_start(par_avg[:], params).then_inc(par_in, DMA)
            act.dma_start(w_all[:], weights).then_inc(w_in, DMA)
            act.wait_ge(b_zero, 1)
            act.dma_start(brow[0:33:32, :], b_qkv).then_inc(b_in, DMA)
            act.dma_start(mats[:], matrices).then_inc(mats_in, DMA)
            act.preload_act_table(ACT.Exp)

            def split_weights():
                act.wait_ge(w_step, 1)
                nc.scalar.activation(w_hi[:], w_f[:], ACT.Copy).then_inc(w_step, 1)

            def affine(j, u):
                p, r, h = at(j, u, 3)
                if not there(p):
                    return
                wait(act, coef_ready, group_of(p) + 1)
                if stacked(p - 2):
                    wait(act, lo_ready, p - 3)
                else:
                    wait(act, q_done, p - 1)
                nc.scalar.activation(xn[:, r, :], x_sb[:, p, :], ACT.Identity, bias=of(coef_b, p),
                                     scale=of(coef_a, p)).then_inc(xn_ready, 1)

            def high_part(j, u):
                p, r, h = at(j, u, 3)
                if not stacked(p):
                    return
                wait(act, xn_ready, p + 1)
                wait(act, xt_in[r], 4 * DMA * (h - 1))
                nc.scalar.activation(split[:, r, 0, :], xn[:, r, :], ACT.Copy).then_inc(hi_ready, 1)

            def key_exp(j, u):
                p, r, h = at(j, u, 0)
                if not there(p):
                    return
                wait(act, ksub_ready, p + 1)
                nc.scalar.activation(ek[:, r, :], ek[:, r, :], ACT.Exp).then_inc(kexp_ready, 1)

            def query_exp(j, u):
                p, r, h = at(j, u, 0)
                if not there(p):
                    return
                wait(act, qmax_ready, p + 1)
                wait(act, out_done, p - 1)
                wait(act, rq_ready, p - 1)
                for image in range(2):
                    last = nc.scalar.activation(eq[:, r, image, :], q_ps[:, image, :], ACT.Exp,
                                                bias=nqmax[:, r, image:image + 1],
                                                accum_out=qs[:, r, image:image + 1])
                last.then_inc(qexp_ready, 1)

            def fold_copy(j, u):
                p, r, h = at(j, u, -1)
                if not there(p):
                    return
                wait(act, fold_done, p + 1)
                wait(act, rq_ready, p + 1)
                wait(act, out_done, p - 1)
                for image in range(2):
                    last = nc.scalar.activation(fold[:, r, image, :],
                                                fold_ps[:, image * CHANNELS:(image + 1) * CHANNELS],
                                                ACT.Copy, scale=rq[:, r, image:image + 1])
                last.then_inc(fold_ready, 1)

            def residual(j, u):
                p, r, h = at(j, u, -3)
                if not there(p):
                    return
                wait(act, coef_ready, group_of(p) + 1)
                nc.scalar.activation(skip[:, p, :], x_sb[:, p, :], ACT.Identity, bias=of(rest0, p),
                                     scale=of(coef_p, p))

            def shift_output(j, u):
                p, r, h = at(j, u, -3)
                if not there(p):
                    return
                wait(act, ve_ready, p + 1)
                wait(act, tm_ready, p + 1)
                nc.scalar.activation(tt[:, r, :], o_ps[r][:, 0:PIX], ACT.Identity,
                                     bias=tm[:, r:r + 1],
                                     scale=par[:, GN2_W:GN2_W + 1]).then_inc(tt_ready, 1)

            def step(j, u):
                residual(j, u)
                shift_output(j, u)
                key_exp(j, u)
                affine(j, u)
                query_exp(j, u)
                fold_copy(j, u)
                high_part(j, u)

            affine(-2, 1)
            split_weights()
            affine(-1, 0)
            affine(-1, 1)
            high_part(-1, 1)
            key_exp(0, 0)
            query_exp(0, 0)
            affine(0, 0)
            high_part(0, 0)
            run_pipeline(act, step, 1, (4, 6), PAIRS - 1)
            residual(4, 0)
            residual(4, 1)
            fold_copy(4, 0)
            shift_output(4, 0)
            shift_output(4, 1)
            residual(5, 0)
            shift_output(5, 0)

        @block.tensor
        def _(pe):
            def warm_up(count):
                for n in range(count):
                    nc.tensor.matmul(c_ps[:], ones[:, 0:128], ones[:], start=True, stop=True)

            def group_average(g):
                a, b = GROUPED[g]
                pe.wait_ge(xmv_ready, g + 1)
                wait(pe, coef_ready, g - 1)
                nc.tensor.matmul(gavg_banks[g][:, 0:2 * (b - a)], avg_group,
                                 xmv[:, a:b, :], start=True, stop=True).then_inc(gavg_done, 1)

            def keys_values(j, u):
                p, r, h = at(j, u, 1)
                if not stacked(p):
                    return
                wait(pe, xt_in[r], 4 * DMA * h)
                wait(pe, vs_ready, p - 1)
                for image in range(2):
                    for chunk in range(CHUNKS):
                        nc.tensor.matmul(kv_ps[r][:, image * CHUNKS + chunk, :, :, :], ones[:, 0:128],
                                         bsplit[:, HIDDEN:3 * HIDDEN], start=(chunk == 0), stop=False,
                                         skip_group_check=True)
                    for chunk in range(CHUNKS):
                        pixels = xt[:, r, image, chunk * 128:(chunk + 1) * 128]
                        for w in (w_hi, w_lo):
                            ins = nc.tensor.matmul(kv_ps[r][:, image * CHUNKS + chunk, :, :, :], pixels,
                                                   w[:, HIDDEN:3 * HIDDEN], start=False,
                                                   stop=(chunk == CHUNKS - 1 and w is w_lo),
                                                   skip_group_check=True)
                ins.then_inc(kv_done, 1)

            def queries(j, u):
                p, r, h = at(j, u, 1)
                if not stacked(p):
                    return
                wait(pe, xt_in[r], 4 * DMA * h)
                wait(pe, qexp_ready, p)
                nc.tensor.matmul(q_ps[:, :, :], bsplit[:, 0:HIDDEN],
                                 ones[:].rearrange("p (i n) -> p i n", i=2), start=True, stop=False,
                                 skip_group_check=True)
                for w in (w_hi, w_lo):
                    ins = nc.tensor.matmul(q_ps[:, :, :], w[:, 0:HIDDEN], xt[:, r, :, :], start=False,
                                           stop=(w is w_lo), skip_group_check=True)
                ins.then_inc(q_done, 1)

            def context(j, u):
                p, r, h = at(j, u, -1)
                if not there(p):
                    return
                wait(pe, vs_ready, p + 1)
                wait(pe, fold_ready, p)
                for blk in range(BLOCKS):
                    image, chunk = divmod(blk, CHUNKS)
                    cols = slice(blk * HIDDEN, (blk + 1) * HIDDEN)
                    ins = nc.tensor.matmul(ctx_ps[:, image * HIDDEN:(image + 1) * HIDDEN],
                                           vs[:, r, cols], ek[:, r, cols],
                                           start=(blk == 0), stop=(chunk == CHUNKS - 1), skip_group_check=True)
                ins.then_inc(ctx_done, 1)

            def folds(j, u):
                p, r, h = at(j, u, -1)
                if not there(p):
                    return
                wait(pe, ctxm_ready, p + 1)
                for image in range(2):
                    ins = nc.tensor.matmul(fold_ps[:, image * CHANNELS:(image + 1) * CHANNELS],
                                           ctxm[:, image, :], wo_sb[:], start=False, stop=True,
                                           skip_group_check=True)
                ins.then_inc(fold_done, 1)

            def outputs(j, u):
                p, r, h = at(j, u, -2)
                if not there(p):
                    return
                wait(pe, fold_ready, p + 1)
                for image in range(2):
                    ins = nc.tensor.matmul(o_ps[r][image * CHANNELS:(image + 1) * CHANNELS, 0:PIX],
                                           fold[:, r, image, :], eq[:, r, image, :], start=True, stop=True)
                ins.then_inc(out_done, 1)

            def centre(j, u):
                p, r, h = at(j, u, -2)
                if not there(p):
                    return
                wait(pe, omv_ready, p + 1)
                nc.tensor.matmul(o_ps[r][:, MEAN:MEAN + 1], mats[:, CENTER, :], omv[:, r, 0:1],
                                 start=True, stop=True).then_inc(cen_done, 1)

            def variance(j, u):
                p, r, h = at(j, u, -3)
                if not there(p):
                    return
                wait(pe, msq_ready, p + 1)
                nc.tensor.matmul(o_ps[r][:, VAR:VAR + 1], mats[:, AVG_IMAGE, :], msq[:, r:r + 1],
                                 start=True, stop=True).then_inc(var_done, 1)

            def step(j, u):
                variance(j, u)
                outputs(j, u)
                context(j, u)
                keys_values(j, u)
                folds(j, u)
                centre(j, u)
                queries(j, u)

            def direct_keys_values(p):
                pe.wait_ge(xn_ready, p + 1)
                pe.wait_ge(w_step, 1)
                for image in (1, 0):
                    for chunk in range(CHUNKS):
                        ins = nc.tensor.matmul(kv_ps[p][:, image * CHUNKS + chunk, :, :, :],
                                               xn[rows(image), p, chunk * 128:(chunk + 1) * 128],
                                               w_f[rows(image), HIDDEN:3 * HIDDEN], start=(chunk == 0),
                                               stop=False, skip_group_check=True)
                    if image == 1:
                        ins.then_inc(image1_done, 1)

            def direct_bias(p):
                pe.wait_ge(b_ready, 1)
                for blk in range(BLOCKS):
                    if blk == CHUNKS:
                        pe.wait_ge(image1_done, 2 * p + 1)
                    ins = nc.tensor.matmul(kv_ps[p][:, blk, :, :, :], ones[:, 0:128],
                                           bsplit[:, HIDDEN:3 * HIDDEN], start=False,
                                           stop=(blk % CHUNKS == CHUNKS - 1), skip_group_check=True)
                ins.then_inc(kv_done, 1)

            def direct_queries_1(p):
                wait(pe, qexp_ready, p)
                nc.tensor.matmul(q_ps[:, 1, :], w_f[rows(1), 0:HIDDEN], xn[rows(1), p, :],
                                 start=True, stop=False, skip_group_check=True).then_inc(image1_done, 1)

            def direct_queries_0(p):
                pe.wait_ge(image1_done, 2 * p + 2)
                nc.tensor.matmul(q_ps[:, 0, :], w_f[rows(0), 0:HIDDEN], xn[rows(0), p, :],
                                 start=False, stop=False, skip_group_check=True)
                nc.tensor.matmul(q_ps[:, :, :], bsplit[:, 0:HIDDEN],
                                 ones[:].rearrange("p (i n) -> p i n", i=2), start=False, stop=True,
                                 skip_group_check=True).then_inc(q_done, 1)

            pe.wait_ge(ones_ready, 1)
            warm_up(5)
            pe.wait_ge(par_in, DMA)
            group_average(0)
            warm_up(6)
            group_average(1)
            warm_up(2)
            direct_keys_values(0)
            direct_queries_1(0)
            direct_bias(0)
            direct_queries_0(0)
            group_average(2)
            warm_up(2)
            direct_keys_values(1)
            direct_bias(1)
            warm_up(2)
            direct_queries_1(1)
            direct_queries_0(1)
            group_average(3)
            pe.wait_ge(mats_in, DMA)
            pe.wait_ge(coef_ready, 3)
            nc.tensor.matmul(o_ps[0][:, 0:1], mats[:, CENTER, :], par[:, OUT_B:OUT_B + 1],
                             start=True, stop=True).then_inc(obc_done, 1)
            warm_up(4)
            pe.wait_ge(w_ready, 1)
            step(0, 1)
            pe.wait_ge(coef_ready, len(GROUPED))
            pe.wait_ge(obc_ready, 1)
            run_pipeline(pe, step, 2, (3, 7), PAIRS - 2)
            outputs(3, 1)
            variance(3, 1)
            context(3, 1)
            folds(3, 1)
            outputs(4, 0)
            context(4, 0)
            centre(3, 1)
            centre(4, 0)
            folds(4, 0)
            variance(4, 0)
            variance(4, 1)
            pe.wait_ge(tt_ready, PAIRS - 2)
            outputs(4, 1)
            centre(4, 1)
            variance(5, 0)

        @block.vector
        def _(dve):
            def raw_stats(g, first, last):
                dve.wait_ge(x_in[g], DMA)
                for p in range(first, last):
                    nc.vector.bn_stats(xstat[:, p, :], x_sb[:, p, :]).then_inc(xstat_ready, 1)

            def channel_moments(g):
                a, b = GROUPED[g]
                for p in range(a, b):
                    dve.wait_ge(xstat_ready, p + 1)
                    ins = nc.vector.bn_aggr(xmv[:, p, :], xstat[:, p, :])
                ins.then_inc(xmv_ready, 1)

            def group_variance(g):
                a, b = GROUPED[g]
                avg = gavg_banks[g][:, 0:2 * (b - a)].rearrange("p (a t) -> p a t", t=2)
                s = GN_STEPS * g
                dve.wait_ge(gavg_done, g + 1)
                nc.vector.tensor_tensor(dev[:, a:b], xmv[:, a:b, 0], avg[:, :, 0],
                                        ALU.subtract).then_inc(gn_step, 1)
                dve.wait_ge(gn_step, s + 1)
                nc.vector.tensor_tensor(dev2[:, a:b], dev[:, a:b], dev[:, a:b], ALU.mult).then_inc(gn_step, 1)
                dve.wait_ge(gn_step, s + 2)
                nc.vector.tensor_tensor(gvar[:, a:b], dev2[:, a:b], avg[:, :, 1], ALU.add).then_inc(gn_step, 1)
                dve.wait_ge(gn_step, s + 3)
                nc.vector.tensor_scalar(pow_in[:, a:b, 0], gvar[:, a:b], EPS, None, ALU.add)
                nc.vector.tensor_scalar(pow_in[:, a:b, 1], gvar[:, a:b], 1.0 + EPS, EPS * EPS,
                                        ALU.mult, ALU.add).then_inc(pow_ready, 1)

            def group_coefficients(g):
                a, b = GROUPED[g]
                avg = gavg_banks[g][:, 0:2 * (b - a)].rearrange("p (a t) -> p a t", t=2)
                s = GN_STEPS * g
                dve.wait_ge(rstd_ready, g + 1)
                dve.wait_ge(par_in, DMA)
                nc.vector.tensor_scalar(coef_a[:, a:b], rstd[:, a:b, 1], par[:, GN1_W:GN1_W + 1], None,
                                        ALU.mult).then_inc(gn_step, 1)
                nc.vector.tensor_scalar(coef_p[:, a:b], rstd[:, a:b, 0], 1.0, None, ALU.add)
                nc.vector.tensor_tensor(mean_r[:, a:b], rstd[:, a:b, 0], avg[:, :, 0],
                                        ALU.mult).then_inc(gn_step, 1)
                dve.wait_ge(gn_step, s + 5)
                nc.vector.tensor_tensor(mean_a[:, a:b], coef_a[:, a:b], avg[:, :, 0],
                                        ALU.mult).then_inc(gn_step, 1)
                nc.vector.tensor_scalar(rest0[:, a:b], mean_r[:, a:b], -1.0, par[:, GN2_B:GN2_B + 1],
                                        ALU.mult, ALU.add)
                dve.wait_ge(gn_step, s + 6)
                nc.vector.tensor_scalar(coef_b[:, a:b], mean_a[:, a:b], -1.0, par[:, GN1_B:GN1_B + 1],
                                        ALU.mult, ALU.add).then_inc(coef_ready, 1)

            def prepare_weights():
                dve.wait_ge(w_in, DMA)
                nc.vector.tensor_scalar(w_f[:, 0:HIDDEN], w_f[:, 0:HIDDEN], QSCALE, None,
                                        ALU.mult).then_inc(w_step, 1)

            def scale_bias():
                dve.wait_ge(b_in, DMA)
                nc.vector.tensor_scalar(brow[:, 0:HIDDEN], brow[:, 0:HIDDEN], QSCALE, None,
                                        ALU.mult).then_inc(b_step, 1)

            def bias_high():
                dve.wait_ge(b_step, 1)
                nc.vector.tensor_copy(bsplit[:], brow[:]).then_inc(b_step, 1)

            def bias_low():
                dve.wait_ge(b_step, 2)
                nc.vector.tensor_tensor(bsplit[32:33, :], brow[32:33, :], bsplit[32:33, :].bitcast(F32),
                                        ALU.subtract).then_inc(b_ready, 1)

            def keys_of(r):
                return kv_ps[r][:, :, 0, :, :]

            def values_of(r):
                return kv_ps[r][:, :, 1, :, :]

            def per_head(t):
                return t.rearrange("p (b g d) -> p b g d", b=BLOCKS, g=HEADS)

            def spread(t):
                return t.rearrange("p (b g) -> p b g", b=BLOCKS).unsqueeze(3).broadcast_to(
                    [128, BLOCKS, HEADS, DIM])

            def key_max(j, u):
                p, r, h = at(j, u, 0)
                if not there(p):
                    return
                wait(dve, kv_done, p + 1)
                wait(dve, ksub_ready, p)
                nc.vector.tensor_reduce(kmx[:], keys_of(r), AX.X, ALU.max).then_inc(kmax_ready, 1)

            def key_shift(j, u):
                p, r, h = at(j, u, 0)
                if not there(p):
                    return
                wait(dve, kmax_ready, p + 1)
                wait(dve, ctx_done, p - 1)
                nc.vector.tensor_tensor(per_head(ek[:, r, :]), keys_of(r), spread(kmx[:]),
                                        ALU.subtract).then_inc(ksub_ready, 1)

            def query_max(j, u):
                p, r, h = at(j, u, 0)
                if not there(p):
                    return
                wait(dve, q_done, p + 1)
                nc.vector.tensor_reduce(nqmax[:, r, :], q_ps[:, :, :], AX.X, ALU.max,
                                        negate=True).then_inc(qmax_ready, 1)

            def key_norm(j, u):
                p, r, h = at(j, u, -1)
                if not there(p):
                    return
                wait(dve, ksum_ready, p + 1)
                wait(dve, vs_ready, p)
                nc.vector.reciprocal(rks[:], ks[:, r, :]).then_inc(rks_ready, 1)

            def last_key_sums():
                p = PAIRS - 1
                dve.wait_ge(kexp_ready, p + 1)
                dve.wait_ge(rks_ready, p - 1)
                nc.vector.tensor_reduce(ks[:, p % 2, :], ek[:, p % 2, :].rearrange("p (g d) -> p g d", d=DIM),
                                        AX.X, ALU.add).then_inc(ksum_ready, 1)

            def scale_values(j, u):
                p, r, h = at(j, u, -1)
                if not there(p):
                    return
                wait(dve, rks_ready, p + 1)
                wait(dve, ctx_done, p - 1)
                nc.vector.tensor_tensor(per_head(vs[:, r, :]), values_of(r), spread(rks[:]),
                                        ALU.mult).then_inc(vs_ready, 1)

            def mask_context(j, u):
                p, r, h = at(j, u, -1)
                if not there(p):
                    return
                wait(dve, qexp_ready, p + 1)
                wait(dve, fold_ready, p - 1)
                nc.vector.reciprocal(rq[:, r, :], qs[:, r, :]).then_inc(rq_ready, 1)
                wait(dve, ctx_done, p + 1)
                wait(dve, fold_done, p)
                nc.vector.tensor_tensor(ctxm[:], ctx_ps.rearrange("p (i d) -> p i d", i=2),
                                        mats[:, HEAD_MASK, :].unsqueeze(1).broadcast_to([P, 2, HIDDEN]),
                                        ALU.mult).then_inc(ctxm_ready, 1)

            def output_stats(j, u):
                p, r, h = at(j, u, -2)
                if not there(p):
                    return
                wait(dve, out_done, p + 1)
                wait(dve, omv_ready, p)
                nc.vector.bn_stats(ostat[:], o_ps[r][:, 0:PIX]).then_inc(ostat_ready, 1)

            def output_moments_waits(j, u):
                p, r, h = at(j, u, -2)
                if not there(p):
                    return
                wait(dve, ostat_ready, p + 1)

            def output_moments(j, u):
                p, r, h = at(j, u, -2)
                if not there(p):
                    return
                nc.vector.bn_aggr(omv[:, r, :], ostat[:]).then_inc(omv_ready, 1)

            def deviation(j, u):
                p, r, h = at(j, u, -3)
                if not there(p):
                    return
                wait(dve, obc_ready, 1)
                wait(dve, cen_done, p + 1)
                nc.vector.tensor_tensor(cdev[:, r:r + 1], o_ps[r][:, MEAN:MEAN + 1], obc[:],
                                        ALU.add).then_inc(cdev_ready, 1)

            def squared_deviation(j, u):
                p, r, h = at(j, u, -3)
                if not there(p):
                    return
                wait(dve, cdev_ready, p + 1)

                nc.vector.scalar_tensor_tensor(out=msq[:, r:r + 1], in0=cdev[:, r:r + 1],
                                               scalar=cdev[:, r:r + 1], in1=omv[:, r, 1:2],
                                               op0=ALU.mult, op1=ALU.add).then_inc(msq_ready, 1)
                nc.vector.scalar_tensor_tensor(out=tm[:, r:r + 1], in0=cdev[:, r:r + 1],
                                               scalar=omv[:, r, 0:1], in1=par[:, GN2_W:GN2_W + 1],
                                               op0=ALU.subtract, op1=ALU.mult).then_inc(tm_ready, 1)

            def variance_eps(j, u):
                p, r, h = at(j, u, -3)
                if not there(p):
                    return
                wait(dve, var_done, p + 1)
                nc.vector.tensor_scalar(ve[:, r:r + 1], o_ps[r][:, VAR:VAR + 1], EPS, None,
                                        ALU.add).then_inc(ve_ready, 1)

            def finish_waits(j, u):
                p, r, h = at(j, u, -3)
                if not there(p):
                    return
                wait(dve, tt_ready, p + 1)
                wait(dve, gn2_ready, p + 1)

            def finish(j, u):
                p, r, h = at(j, u, -3)
                if not there(p):
                    return
                nc.vector.scalar_tensor_tensor(out=res[:, p, :], in0=tt[:, r, :], scalar=orstd[:, r:r + 1],
                                               in1=skip[:, p, :], op0=ALU.mult,
                                               op1=ALU.add).then_inc(res_ready, 1)

            def step(j, u):
                key_max(j, u)
                deviation(j, u)
                key_norm(j, u)
                squared_deviation(j, u)
                scale_values(j, u)
                variance_eps(j, u)
                key_shift(j, u)
                query_max(j, u)
                output_stats(j, u)
                mask_context(j, u)
                finish_waits(j, u)
                output_moments_waits(j, u)
                finish(j, u)
                output_moments(j, u)

            raw_stats(0, 0, 1)
            channel_moments(0)
            group_variance(0)
            prepare_weights()
            raw_stats(1, 1, 3)
            channel_moments(1)
            group_coefficients(0)
            group_variance(1)
            scale_bias()
            bias_high()
            bias_low()
            group_coefficients(1)
            raw_stats(2, 3, 5)
            channel_moments(2)
            key_max(0, 0)
            group_variance(2)
            key_shift(0, 0)
            query_max(0, 0)
            group_coefficients(2)
            raw_stats(3, 5, 8)
            channel_moments(3)
            key_max(0, 1)
            key_norm(0, 1)
            group_variance(3)
            scale_values(0, 1)
            key_shift(0, 1)
            query_max(0, 1)
            dve.wait_ge(obc_done, 1)
            nc.vector.tensor_copy(obc[:], o_ps[0][:, 0:1]).then_inc(obc_ready, 1)
            mask_context(0, 1)
            group_coefficients(3)
            run_pipeline(dve, step, 2, (3, 7), PAIRS - 2)
            key_max(3, 1)
            deviation(3, 1)
            key_norm(3, 1)
            squared_deviation(3, 1)
            scale_values(3, 1)
            variance_eps(3, 1)
            key_shift(3, 1)
            query_max(3, 1)
            mask_context(3, 1)
            last_key_sums()
            output_stats(3, 1)
            output_moments_waits(3, 1)
            key_norm(4, 0)
            output_moments(3, 1)
            scale_values(4, 0)
            output_stats(4, 0)
            output_moments_waits(4, 0)
            output_moments(4, 0)
            finish_waits(3, 1)
            finish(3, 1)
            mask_context(4, 0)
            deviation(4, 0)
            deviation(4, 1)
            squared_deviation(4, 0)
            squared_deviation(4, 1)
            variance_eps(4, 0)
            variance_eps(4, 1)
            finish_waits(4, 0)
            finish(4, 0)
            output_stats(4, 1)
            output_moments_waits(4, 1)
            output_moments(4, 1)
            finish_waits(4, 1)
            finish(4, 1)
            deviation(5, 0)
            squared_deviation(5, 0)
            variance_eps(5, 0)
            finish_waits(5, 0)
            finish(5, 0)


GN_STEPS = 6


def kernel(**inputs):
    import concourse.bacc as bacc
    from concourse.bass_utils import run_bass_kernel_spmd

    arr = {k: np.ascontiguousarray(v) for k, v in inputs.items()}
    names = ("gn1_w", "gn1_b", "out_b", "gn2_w", "gn2_b")
    params = np.stack([np.concatenate([arr["L0_conv_" + n]] * 2) for n in names], axis=1)
    c = np.arange(P)
    group = (c[:, None] // GROUP_CH == c[None, :] // GROUP_CH) / GROUP_CH
    image = (c[:, None] // CHANNELS == c[None, :] // CHANNELS) / CHANNELS
    heads = c[:, None] // DIM == c[None, :] // DIM
    matrices = np.stack([np.eye(P) - image, image, heads], axis=1).astype(np.float32)
    data = {
        "x": arr["x"].reshape(IMAGES, CHANNELS, PIX),
        "params": np.concatenate([params, group.astype(np.float32)], axis=1),
        "weights": np.concatenate([np.concatenate([arr["L0_conv_qkv_w"].T] * 2), arr["L0_conv_out_w"].T], axis=1),
        "b_qkv": np.stack([arr["L0_conv_qkv_b"]] * 2),
        "matrices": matrices,
    }
    nc = bacc.Bacc("TRN2", target_bir_lowering=False, num_devices=1)
    args = [nc.dram_tensor(n + "_dram", a.shape, mybir.dt.from_np(a.dtype), kind="ExternalInput").ap()
            for n, a in data.items()]
    out = nc.dram_tensor("out_dram", (IMAGES, CHANNELS, PIX), F32, kind="ExternalOutput").ap()
    attention_kernel(nc, *args, out)
    r = run_bass_kernel_spmd(nc, [{n + "_dram": a for n, a in data.items()}], core_ids=[0])
    return r.results[0]["out_dram"].reshape(IMAGES, CHANNELS, SIDE, SIDE)
```
